# Optimizing a Trainium2 kernel written in Bass

```python
import numpy as np
import jax
import jax.numpy as jnp

def _softmax(x, axis=-1):
    return jax.nn.softmax(x, axis=axis)

def _gelu(x):
    return jax.nn.gelu(x, approximate=True)

def _silu(x):
    return jax.nn.silu(x)

def _sigmoid(x):
    return jax.nn.sigmoid(x)

def _layernorm(x, axis=-1, eps=1e-05):
    m = jnp.mean(x, axis=axis, keepdims=True)
    v = jnp.var(x, axis=axis, keepdims=True)
    return (x - m) / jnp.sqrt(v + eps)

def _scatter_add(tgt, idx, src, axis=0):
    return tgt.at[idx].add(src)

def _segment_sum(src, seg, n):
    return jax.ops.segment_sum(src, seg, n)
kernel_name = 'mk_seq_postln_d1_jaxref_r4_fa05a4'

def setup_inputs(seed: int=0):
    np.random.seed(seed)
    _w = jnp.asarray

    def _L0_attn_setup():
        import jax, jax.numpy as jnp
        import numpy as np
        D_MODEL = 256
        NHEAD = 16
        HEAD_DIM = D_MODEL // NHEAD

        def _rope(x, sin, cos):
            half = x.shape[-1] // 2
            x1, x2 = (x[..., :half], x[..., half:])
            rotated = jnp.concatenate([-x2, x1], axis=-1)
            return x * cos + rotated * sin
        key = jax.random.key(seed)
        ks = jax.random.split(key, 9)
        s = 0.02
        x = jax.random.normal(ks[0], (2, 512, D_MODEL), dtype=jnp.float32)
        Wq = jax.random.normal(ks[1], (D_MODEL, D_MODEL), dtype=jnp.float32) * s
        bq = jnp.zeros((D_MODEL,), jnp.float32)
        Wk = jax.random.normal(ks[2], (D_MODEL, D_MODEL), dtype=jnp.float32) * s
        bk = jnp.zeros((D_MODEL,), jnp.float32)
        Wv = jax.random.normal(ks[3], (D_MODEL, D_MODEL), dtype=jnp.float32) * s
        bv = jnp.zeros((D_MODEL,), jnp.float32)
        Wo = jax.random.normal(ks[4], (D_MODEL, D_MODEL), dtype=jnp.float32) * s
        bo = jnp.zeros((D_MODEL,), jnp.float32)
        return {'x': x, 'Wq': Wq, 'bq': bq, 'Wk': Wk, 'bk': bk, 'Wv': Wv, 'bv': bv, 'Wo': Wo, 'bo': bo}
    _L0_attn_in = _L0_attn_setup()

    def _L0_ffn_setup():
        import jax, jax.numpy as jnp
        from jax import lax
        import numpy as np
        D_MODEL = 256
        HIDDEN = 128
        N_EXPERTS = 32
        TOP_K = 2
        B, S = (1, 1024)

        def _moe_group(x2, router_w, wg, wu, wd, top_k):
            T = x2.shape[0]
            n_experts = router_w.shape[1]
            logits = x2 @ router_w
            scores = jax.nn.softmax(logits, axis=-1)
            expert_weights, expert_indices = lax.top_k(scores, top_k)
            flat_e = expert_indices.reshape(-1)
            flat_w = expert_weights.reshape(-1)
            flat_t = jnp.repeat(jnp.arange(T), top_k)
            order = jnp.argsort(flat_e)
            tok = flat_t[order]
            xs = x2[tok]
            group_sizes = jnp.bincount(flat_e, length=n_experts).astype(jnp.int32)
            gate = lax.ragged_dot(xs, wg, group_sizes)
            up = lax.ragged_dot(xs, wu, group_sizes)
            ys = lax.ragged_dot(jax.nn.silu(gate) * up, wd, group_sizes)
            ys = ys * flat_w[order][:, None]
            return jnp.zeros_like(x2).at[tok].add(ys)
        key = jax.random.key(seed)
        ks = jax.random.split(key, 9)
        w = lambda k, shape: jax.random.normal(k, shape, dtype=jnp.float32) * 0.02
        return {'x': jax.random.normal(ks[0], (B, S, D_MODEL), dtype=jnp.float32), 'router_w0': w(ks[1], (D_MODEL, N_EXPERTS)), 'wg0': w(ks[2], (N_EXPERTS, D_MODEL, HIDDEN)), 'wu0': w(ks[3], (N_EXPERTS, D_MODEL, HIDDEN)), 'wd0': w(ks[4], (N_EXPERTS, HIDDEN, D_MODEL)), 'router_w1': w(ks[5], (D_MODEL, N_EXPERTS)), 'wg1': w(ks[6], (N_EXPERTS, D_MODEL, HIDDEN)), 'wu1': w(ks[7], (N_EXPERTS, D_MODEL, HIDDEN)), 'wd1': w(ks[8], (N_EXPERTS, HIDDEN, D_MODEL))}
    _L0_ffn_in = _L0_ffn_setup()
    _d = {'L0_attn_x': _L0_attn_in['x'], 'L0_attn_Wq': _L0_attn_in['Wq'], 'L0_attn_bq': _L0_attn_in['bq'], 'L0_attn_Wk': _L0_attn_in['Wk'], 'L0_attn_bk': _L0_attn_in['bk'], 'L0_attn_Wv': _L0_attn_in['Wv'], 'L0_attn_bv': _L0_attn_in['bv'], 'L0_attn_Wo': _L0_attn_in['Wo'], 'L0_attn_bo': _L0_attn_in['bo'], 'L0_ffn_router_w0': _L0_ffn_in['router_w0'], 'L0_ffn_wg0': _L0_ffn_in['wg0'], 'L0_ffn_wu0': _L0_ffn_in['wu0'], 'L0_ffn_wd0': _L0_ffn_in['wd0'], 'L0_ffn_router_w1': _L0_ffn_in['router_w1'], 'L0_ffn_wg1': _L0_ffn_in['wg1'], 'L0_ffn_wu1': _L0_ffn_in['wu1'], 'L0_ffn_wd1': _L0_ffn_in['wd1']}
    _x0 = _d['L0_attn_x']
    _d['L0_attn_x'] = jax.random.normal(jax.random.fold_in(jax.random.key(seed), 1), (8, 1024, 256), dtype=_x0.dtype)
    del _x0
    return _d

def reference(L0_attn_x, L0_attn_Wq, L0_attn_bq, L0_attn_Wk, L0_attn_bk, L0_attn_Wv, L0_attn_bv, L0_attn_Wo, L0_attn_bo, L0_ffn_router_w0, L0_ffn_wg0, L0_ffn_wu0, L0_ffn_wd0, L0_ffn_router_w1, L0_ffn_wg1, L0_ffn_wu1, L0_ffn_wd1):

    def _L0_attn_ref(x, Wq, bq, Wk, bk, Wv, bv, Wo, bo):
        import jax, jax.numpy as jnp
        import numpy as np
        D_MODEL = 256
        NHEAD = 16
        HEAD_DIM = D_MODEL // NHEAD

        def _rope(x, sin, cos):
            half = x.shape[-1] // 2
            x1, x2 = (x[..., :half], x[..., half:])
            rotated = jnp.concatenate([-x2, x1], axis=-1)
            return x * cos + rotated * sin
        B, L, D = x.shape
        H, Dh = (NHEAD, HEAD_DIM)
        q = (x @ Wq.T + bq).reshape(B, L, H, Dh)
        k = (x @ Wk.T + bk).reshape(B, L, H, Dh)
        v = (x @ Wv.T + bv).reshape(B, L, H, Dh)
        inv_freq = 1.0 / 10000.0 ** (jnp.arange(0, Dh, 2, dtype=jnp.float32) / Dh)
        t = jnp.arange(L, dtype=jnp.float32)
        freqs = jnp.einsum('i,j->ij', t, inv_freq)
        emb = jnp.concatenate([freqs, freqs], axis=-1)
        cos = jnp.cos(emb)[None, :, None, :]
        sin = jnp.sin(emb)[None, :, None, :]
        q = _rope(q, sin, cos)
        k = _rope(k, sin, cos)
        scores = jnp.einsum('bqhd,bkhd->bhqk', q, k) / jnp.sqrt(jnp.float32(Dh))
        attn = jax.nn.softmax(scores, axis=-1)
        out = jnp.einsum('bhqk,bkhd->bqhd', attn, v).reshape(B, L, D)
        return out @ Wo.T + bo

    def _L0_ffn_ref(x, router_w0, wg0, wu0, wd0, router_w1, wg1, wu1, wd1):
        import jax, jax.numpy as jnp
        from jax import lax
        import numpy as np
        D_MODEL = 256
        HIDDEN = 128
        N_EXPERTS = 32
        TOP_K = 2
        B, S = (1, 1024)

        def _moe_group(x2, router_w, wg, wu, wd, top_k):
            T = x2.shape[0]
            n_experts = router_w.shape[1]
            logits = x2 @ router_w
            scores = jax.nn.softmax(logits, axis=-1)
            expert_weights, expert_indices = lax.top_k(scores, top_k)
            flat_e = expert_indices.reshape(-1)
            flat_w = expert_weights.reshape(-1)
            flat_t = jnp.repeat(jnp.arange(T), top_k)
            order = jnp.argsort(flat_e)
            tok = flat_t[order]
            xs = x2[tok]
            group_sizes = jnp.bincount(flat_e, length=n_experts).astype(jnp.int32)
            gate = lax.ragged_dot(xs, wg, group_sizes)
            up = lax.ragged_dot(xs, wu, group_sizes)
            ys = lax.ragged_dot(jax.nn.silu(gate) * up, wd, group_sizes)
            ys = ys * flat_w[order][:, None]
            return jnp.zeros_like(x2).at[tok].add(ys)
        b, s, d = x.shape
        x2 = x.reshape(-1, d)
        out0 = _moe_group(x2, router_w0, wg0, wu0, wd0, TOP_K)
        out1 = _moe_group(x2, router_w1, wg1, wu1, wd1, TOP_K)
        out = (out0 * TOP_K + out1 * TOP_K) / (TOP_K + TOP_K)
        return out.reshape(b, s, d)
    x = L0_attn_x
    x = _layernorm(x + _L0_attn_ref(x, L0_attn_Wq, L0_attn_bq, L0_attn_Wk, L0_attn_bk, L0_attn_Wv, L0_attn_bv, L0_attn_Wo, L0_attn_bo), axis=-1)
    x = _layernorm(x + _L0_ffn_ref(x, L0_ffn_router_w0, L0_ffn_wg0, L0_ffn_wu0, L0_ffn_wd0, L0_ffn_router_w1, L0_ffn_wg1, L0_ffn_wu1, L0_ffn_wd1), axis=-1)
    return x

_drawn_inputs = setup_inputs


def setup_inputs(seed=0):
    import zlib

    import numpy as np

    out = dict(_drawn_inputs(seed))
    spreads = {'L0_attn_bq': (0.0, 0.8),
     'L0_attn_bk': (0.0, 0.8),
     'L0_attn_bv': (0.0, 0.1),
     'L0_attn_bo': (0.0, 0.1)}
    factors = {'L0_attn_Wq': 8.0,
     'L0_attn_Wk': 8.0,
     'L0_attn_Wv': 8.0,
     'L0_ffn_router_w0': 8.0,
     'L0_ffn_wg0': 8.0,
     'L0_ffn_wu0': 8.0,
     'L0_ffn_wd0': 8.0,
     'L0_ffn_router_w1': 8.0,
     'L0_ffn_wg1': 8.0,
     'L0_ffn_wu1': 8.0,
     'L0_ffn_wd1': 8.0}
    for name, (base, spread) in spreads.items():
        noise = np.random.default_rng([zlib.crc32(name.encode()), seed]).standard_normal(out[name].shape)
        drawn = base * np.exp(spread * noise) if base else spread * noise
        out[name] = jnp.asarray(drawn.astype(out[name].dtype))
    for name, factor in factors.items():
        out[name] = (out[name] * factor).astype(out[name].dtype)
    return out
```

```python
import numpy as np
import concourse.bass as bass
from concourse import mybir
from contextlib import ExitStack

F32, BF16, I32, U32 = mybir.dt.float32, mybir.dt.bfloat16, mybir.dt.int32, mybir.dt.uint32
ALU, ACT, AX = mybir.AluOpType, mybir.ActivationFunctionType, mybir.AxisListType

P = 128
L, D, H, DH = 1024, 256, 16, 16
DC = D // P
G = 4
HALF = 512
KC = L // P
UPB = H // G
STEPS = (L // HALF) * KC
SPB = UPB * STEPS
LEAD = STEPS + 6
NPART, NTERM = 3, 6
Q_PART, Q_RUNS = (0, 0, 0, 1, 1, 2), ((0, 0, 1), (1, 0, 1), (2, 0, 2), (4, 1, 2))
K_PART, K_RUNS = (0, 1, 2, 0, 1, 0), ((0, 0, 3), (3, 0, 2), (5, 0, 1))
ROWS = NTERM * DH
XROWS = ROWS + NPART
STACK_DMAS = len(Q_RUNS) + len(K_RUNS)
NSTK = 3
EPS = 1e-5
NE, HID, NG, TOPK = 32, 128, 2, 2
RSQRT_SEED = 0x5F3759DF


def n_tiles(tokens):
    return (tokens * TOPK + NE * (P - 1)) // P


def const_layout(tiles):
    at, out = 0, {}
    for name, width in (("ident", P), ("tri", P), ("iota", max(tiles, P)),
                        ("scan", NG * NE * KC), ("pid", 1)):
        out[name] = (at, width)
        at += width
    return out, at


def schedule(nb):
    jobs = []
    for b in range(nb):
        start, end = SPB * b, SPB * (b + 1)
        for i, (what, half) in enumerate((("Q", 0), ("Q", 1), ("K", 0), ("K", 1))):
            for c, at in enumerate((start - 46, start - 20)):
                jobs.append((at + 2 * i, what, (b, c, half)))
        for i in range(KC // 2):
            jobs.append((start - 8 + 2 * i, "V", (b, i)))
            jobs.append((end + (12, 13, 15, 16)[i], "O", (b, i)))
            jobs.append((end + 26 + 2 * i, "T", (b, i)))
            jobs.append((end + 27 + 2 * i, "L", (b, i)))
        for u in range(UPB):
            jobs.append((start + STEPS * u - 5, "M", (UPB * b + u,)))
        jobs.append((end + 54, "S", (b,)))
        jobs.append((end + 55, "R", (b,)))
    order = {n: i for i, n in enumerate("MQKVOTLSR")}
    jobs.sort(key=lambda j: (j[0], order[j[1]]))
    return jobs


LONG_JOBS = "QKVO"
VEC_COST = {
    "max_parts": [1] * 5,
    "recip": [6],
    "norm": [3] * KC + [1] * (KC + 3 + 9) + [3] * KC,
    "top2": [1] * KC * NG + [6, 1] + [1] * KC * NG,
    "route": [6, 1, 1, 1, 1, 1, 6, 6],
    "ranks": [6] * 9,
}


def attention_phase(nc, nb, dram, keep, k):
    jobs = schedule(nb)
    job_no = {(name, args): n for n, (_, name, args) in enumerate(jobs)}
    at_step = {}
    for n, (t, name, args) in enumerate(jobs):
        at_step.setdefault(t, []).append((n, name, args))
    n_steps = SPB * nb
    first, last = min(at_step), max(at_step)
    n_units = UPB * nb

    with ExitStack() as ctx:
        sb = lambda name, shape, dt=F32: ctx.enter_context(nc.sbuf_tensor(name + "_sb", shape, dt))
        ps = lambda name, shape: ctx.enter_context(nc.psum_tensor(name, shape, F32))
        sem = lambda name: ctx.enter_context(nc.semaphore(name))

        x_t = sb("x_t", [P, DC, L])
        w_q, w_k, w_v, w_o = (sb(n, [P, DC, D]) for n in ("w_q", "w_k", "w_v", "w_o"))
        bias = sb("bias", [P, 3, DC])
        bo_row = sb("bo_row", [P, D])
        trig = sb("trig", [P, 2, L])
        router = sb("router", [P, DC, NG * NE])
        feat = [sb(f"feat_{n}", [P, L]) for n in "qk"]
        swapped = sb("swapped", [P, L])
        parts = [sb(f"parts_{n}", [P, NPART, L], BF16) for n in "qk"]
        q_stack = [sb(f"q_stack{i}", [P, G, L], BF16) for i in range(NSTK)]
        k_stack = [sb(f"k_stack{i}", [P, G, L], BF16) for i in range(NSTK)]
        v_sb = [sb(f"v_sb{i}", [P, KC * D, 2]) for i in range(2)]
        probs = [sb(f"probs{i}", [P, G, HALF]) for i in range(2)]
        maxima = [sb(f"maxima{i}", [P, G * KC, 2]) for i in range(2)]
        neg_max = sb("neg_max", [P, G * KC])
        max_rest = sb("max_rest", [P, G * KC])
        max_parts = sb("max_parts", [P, NPART, G * KC], BF16)
        max_rows = sb("max_rows", [NPART * G * KC, P], BF16)
        o_raw = [sb(f"o_raw{i}", [P, HALF]) for i in range(2)]
        o_feat = [sb(f"o_feat{i}", [P, DC, L]) for i in range(2)]
        o_den = sb("o_den", [P, DC, L])
        den = sb("den", [P, H * L // P])
        y = sb("y", [P, KC, D])
        stats, mean_var = sb("stats", [P, KC, 6]), sb("mean_var", [P, KC, 2])
        rstd, half_var, newton = (sb(n, [P, KC]) for n in ("rstd", "half_var", "newton"))
        x1_t = [sb(f"x1_t{i}", [P, 2, DC, P]) for i in range(2)]
        logits = sb("logits", [P, KC * NG, NE])
        top_val = sb("top_val", [P, KC * NG, 8])
        top_idx = sb("top_idx", [P, KC * NG, 8], U32)
        shifted = sb("shifted", [P, KC * NG * NE + KC * NG])
        exps = shifted
        denom = sb("denom", [P, KC * NG])
        hot = [sb(f"hot{i}", [P, NG, KC, NE], BF16) for i in range(TOPK)]
        totals, incl = (sb(n, [P, NG * NE * KC]) for n in ("totals", "incl"))
        rank_of = logits[:, :, :].rearrange("p a e -> p (a e)")
        ident_bf, tri_bf, ones_bf = (sb(n, [P, P], BF16) for n in ("ident_bf", "tri_bf", "ones_bf"))

        ps_b = [ps(f"ps_b{i}", [P, 2, HALF]) for i in range(2)]
        ps_a = [ps(f"ps_a{i}", [P, HALF]) for i in range(2)]
        ps_o = ps("ps_o", [P, HALF])
        ps_j = ps("ps_j", [P, HALF])

        s_par, s_xt, s_y = sem("parameters_in"), sem("x_t_in"), sem("y_in")
        s_set, s_ones = sem("constants_made"), sem("ones_made")
        s_fill, s_drain = sem("job_filled"), sem("job_drained")
        s_score, s_exp, s_pv = sem("scored"), sem("exponentiated"), sem("pv_done")
        s_a, s_amax = sem("a_scored"), sem("a_maximum")
        s_den = sem("den_moved")
        s_oraw = [sem(f"o_raw_out{i}") for i in range(2)]
        s_ocp = sem("o_copied")
        s_swap, s_parts = sem("swapped_in"), sem("parts_out")
        s_pool = sem("pool_step")
        s_stack = [sem(f"stack_in{i}") for i in range(NSTK)]
        s_mrow = sem("max_rows_in")
        s_v = sem("vector_step")
        s_x1 = sem("x1_out")
        s_eexp = sem("router_exp")
        block = ctx.enter_context(nc.Block())

        consts = keep["consts"]
        con = lambda name: consts[:, k["cols"][name][0]:k["cols"][name][0] + k["cols"][name][1]]

        pool_no = {}

        def pool_plan():
            todo = []
            for b in range(nb):
                for c in range(DC):
                    at = job_step[("K", (b, c, 1))]
                    todo.append((at, "split", (b, c)))
                todo.append((SPB * b + 40, "bias_y", (b,)))
                todo.append((SPB * (b + 1) + 4, "norm_o", (b,)))
            todo.sort(key=lambda x: x[0])
            return todo

        job_step = {(name, args): t for t, name, args in jobs}
        todo_pool = pool_plan()
        POOL_STEPS = {"split": 14, "bias_y": 1, "norm_o": 2 * DC}
        count = 0
        for _, name, args in todo_pool:
            pool_no[(name, args)] = count
            count += POOL_STEPS[name]

        vec_tasks = [(STEPS * u - 6, 0, "max_parts", (u,)) for u in range(n_units)]
        for b in range(nb):
            end = SPB * (b + 1)
            vec_tasks += [(end + 3, 1, "recip", (b,)), (end + 17, 2, "norm", (b,)), (end + 34, 3, "top2", (b,)),
                          (end + 47, 4, "route", (b,)), (end + 56, 5, "ranks", (b,))]
        vec_tasks.sort()
        VEC_STEPS = {name: len(cost) for name, cost in VEC_COST.items()}
        steps_end = max(last, vec_tasks[-1][0], n_steps) + 1
        vec_deal, vec_last, vec_step = {}, {}, {}
        waiting, left, dealt = list(vec_tasks), {}, 0
        for t in range(first, steps_end):
            for slot in range(4):
                if not 0 <= t + LEAD < n_steps:
                    room = 1 << 30
                elif slot < 3:
                    room = 0
                else:
                    room = 18 if any(name in LONG_JOBS for at in (t, t - SPB) for _, name, _ in at_step.get(at, [])) else 3
                while True:
                    ready = [x for x in waiting if x[0] <= t and (room > 0 or x[1] == 0)]
                    if not ready:
                        break
                    task = min(ready, key=lambda x: (x[1] != 0, x[0]))
                    key = task[2:]
                    k_op = left.get(key, 0)
                    vec_deal.setdefault((t, slot), []).append((*key, k_op))
                    left[key] = k_op + 1
                    dealt += 1
                    room -= VEC_COST[key[0]][k_op]
                    if k_op + 1 == VEC_STEPS[key[0]]:
                        vec_last[key], vec_step[key] = dealt, t
                        waiting.remove(task)
        assert not waiting
        for t, name, args in jobs:
            before = {"M": "max_parts", "O": "recip", "T": "norm", "S": "route", "R": "route"}.get(name)
            assert before is None or vec_step[(before, args[:1])] <= t, (t, name, args)
        vec_done = lambda name, *args: vec_last[(name, args)]
        pool_done = lambda name, *args: pool_no[(name, args)] + POOL_STEPS[name]

        def wait(eng, s, value):
            if value > 0:
                eng.wait_ge(s, value)

        @block.sync
        def _(sp):
            sp.dma_start(x_t[:, :, :], dram["x_t"][0]).then_inc(s_xt, 16)
            for dst, src in ((w_q, "w_q"), (bias, "bias"), (w_k, "w_k"), (consts, "consts"), (trig, "trig"), (w_v, "w_v"),
                             (w_o, "w_o"), (bo_row, "bo_row"), (router, "router")):
                sp.dma_start(dst[:], dram[src][:]).then_inc(s_par, 16)

            def swap(b, c, which):
                wait(sp, s_drain, job_no[("QK"[which], (b, c, 1))] + 1)
                if which == 1:
                    wait(sp, s_pool, pool_no[("split", (b, c))] + 7)
                elif (b, c) != (0, 0):
                    pb, pc = divmod(b * DC + c - 1, DC)
                    wait(sp, s_pool, pool_done("split", pb, pc))
                for lo, hi in ((0, P // 2), (P // 2, 0)):
                    sp.dma_start(swapped[lo:lo + P // 2, :], feat[which][hi:hi + P // 2, :]).then_inc(s_swap, 16)

            def parts_out(b, c, which):
                wait(sp, s_pool, pool_no[("split", (b, c))] + 7 * (which + 1))
                sp.dma_start(dram["parts"][b * DC + c, which].rearrange("t p l -> p t l"),
                             parts[which][:, :, :]).then_inc(s_parts, 16)

            def stack(u):
                b, g = divmod(u, UPB)
                c = g // 2
                wait(sp, s_parts, 16 * 2 * (b * DC + c + 1))
                wait(sp, s_score, 2 * STEPS * (u - NSTK + 1))
                for stk, which, runs in ((q_stack, 0, Q_RUNS), (k_stack, 1, K_RUNS)):
                    src = dram["parts"][b * DC + c, which].rearrange("t (r j) l -> (t r) j l", j=2 * G)
                    for term, part, n in runs:
                        sp.dma_start(stk[u % NSTK][term * DH:(term + n) * DH, :, :],
                                     src[part * DH:(part + n) * DH, (g % 2) * G:(g % 2 + 1) * G, :]
                                     ).then_inc(s_stack[u % NSTK], 16)

            def max_row(u):
                wait(sp, s_drain, job_no[("M", (u,))] + 1)
                for i in range(NPART):
                    sp.dma_start(q_stack[u % NSTK][ROWS + i:ROWS + i + 1, :, :].rearrange("o j (t q) -> o (j t) q", q=P),
                                 max_rows[i * G * KC:(i + 1) * G * KC, :]).then_inc(s_mrow, 16)

            def o_out(n):
                u, half = divmod(n, 2)
                b, g = divmod(u, UPB)
                wait(sp, s_ocp, n + 1)
                if n % (2 * UPB) == 0:
                    if b >= 2:
                        wait(sp, s_fill, job_no[("O", (b - 2, KC // 2 - 1))] + 1)
                lo = (g % 2) * G * DH
                sp.dma_start(o_feat[b % 2][lo:lo + G * DH, g // 2, half * HALF:(half + 1) * HALF],
                             o_raw[n % 2][0:P:2, :]).then_inc(s_oraw[n % 2], 16)
                sp.dma_start(dram["den"][b, g * G:(g + 1) * G, half * HALF:(half + 1) * HALF],
                             o_raw[n % 2][1:P:2 * DH, :]).then_inc(s_oraw[n % 2], 16)

            def den_in(b):
                for i in range(2):
                    wait(sp, s_oraw[i], 16 * 2 * UPB * (b + 1))
                if b:
                    wait(sp, s_v, vec_done("recip", b - 1))
                    wait(sp, s_den, 16 * (2 + H) * b)
                sp.dma_start(den[:, :], dram["den"][b].rearrange("h (a l) -> (h a) l", a=P // H)).then_inc(s_den, 16)

            def den_out(b):
                wait(sp, s_v, vec_done("recip", b))
                sp.dma_start(dram["inv"][b].rearrange("h (a l) -> (h a) l", a=P // H), den[:, :]).then_inc(s_den, 16)
                if b:
                    wait(sp, s_pool, pool_done("norm_o", b - 1))
                wait(sp, s_den, 16 * ((2 + H) * b + 2))
                for h in range(H):
                    lo = h % (P // DH) * DH
                    sp.dma_start(o_den[lo:lo + DH, h * DH // P, :],
                                 dram["inv"][b, h:h + 1, :].to_broadcast([DH, L])).then_inc(s_den, 16)

            tasks = []
            for b in range(nb):
                for c in range(DC):
                    t = job_step[("K", (b, c, 1))]
                    tasks.append((t - 1, 0, swap, (b, c, 0)))
                    tasks.append((t + 1, 0, swap, (b, c, 1)))
                    tasks.append((t + 4, 0, parts_out, (b, c, 0)))
                    tasks.append((t + 8, 0, parts_out, (b, c, 1)))
                    for g in (2 * c, 2 * c + 1):
                        u = UPB * b + g
                        tasks.append((max(t + 9, STEPS * (u - 2) + 1), 1, stack, (u,)))
            for u in range(n_units):
                tasks.append((STEPS * u - 4.5, 2, max_row, (u,)))
                for half in range(2):
                    tasks.append((STEPS * u + 8 * (half + 1) + 1, 3, o_out, (2 * u + half,)))
            for b in range(nb):
                tasks.append((SPB * b + 36, 4, "y", (b,)))
                tasks.append((SPB * (b + 1) + 2, 4, den_in, (b,)))
                tasks.append((SPB * (b + 1) + 4, 4, den_out, (b,)))
                tasks.append((SPB * (b + 1) + 25, 5, "x1", (b,)))
                if b + 1 < nb:
                    tasks.append((SPB * b + 2, 6, "xt", (b + 1,)))
            tasks.sort(key=lambda x: (x[0], x[1]))
            for _, _, what, args in tasks:
                if what == "xt":
                    b, = args
                    wait(sp, s_fill, max(job_no[("K", (b - 1, 1, 1))], job_no[("V", (b - 1, KC // 2 - 1))]) + 1)
                    sp.dma_start(x_t[:, :, :], dram["x_t"][b]).then_inc(s_xt, 16)
                elif what == "y":
                    b, = args
                    if b:
                        wait(sp, s_x1, 16 * b)
                        wait(sp, s_fill, job_no[("T", (b - 1, KC // 2 - 1))] + 1)
                    sp.dma_start(y[:, :, :], dram["x"][b]).then_inc(s_y, 16)
                elif what == "x1":
                    b, = args
                    wait(sp, s_v, vec_done("norm", b))
                    sp.dma_start(dram["x1"][b * L:(b + 1) * L, :].rearrange("(t p) d -> p t d", p=P),
                                 y[:, :, :]).then_inc(s_x1, 16)
                else:
                    what(*args)
            wait(sp, s_x1, 16 * nb)

        @block.gpsimd
        def _(pool):
            ones = [k_stack[i][ROWS:ROWS + NPART, :, :] for i in range(NSTK)] + [v[:, :, 1] for v in v_sb] + [ones_bf[:, :]]
            for i, dst in enumerate(ones):
                pool.memset(dst, 1.0).then_inc(s_ones, 1)
                pool.wait_ge(s_ones, i + 1)
            done = [0]

            def step(ins, chained=True):
                ins.then_inc(s_pool, 1)
                done[0] += 1
                if chained:
                    pool.wait_ge(s_pool, done[0])

            wait(pool, s_par, 16 * 9)
            for _, name, args in todo_pool:
                assert done[0] == pool_no[(name, args)]
                if name == "split":
                    b, c = args
                    n = b * DC + c
                    wait(pool, s_parts, 16 * 2 * n)
                    for which in range(2):
                        f, part = feat[which], parts[which]
                        wait(pool, s_drain, job_no[("QK"[which], (b, c, 1))] + 1)
                        wait(pool, s_swap, 16 * 2 * (2 * n + which + 1))
                        step(pool.tensor_tensor(f[:, :], f[:, :], trig[:, 0, :], ALU.mult))
                        step(pool.tensor_tensor(swapped[:, :], swapped[:, :], trig[:, 1, :], ALU.mult))
                        step(pool.tensor_tensor(part[:, 0, :], f[:, :], swapped[:, :], ALU.add))
                        step(pool.tensor_tensor(f[:, :], f[:, :], swapped[:, :], ALU.add))
                        step(pool.tensor_tensor(part[:, 1, :], f[:, :], part[:, 0, :], ALU.subtract))
                        step(pool.tensor_tensor(f[:, :], f[:, :], part[:, 0, :], ALU.subtract))
                        step(pool.tensor_tensor(part[:, 2, :], f[:, :], part[:, 1, :], ALU.subtract))
                elif name == "bias_y":
                    b, = args
                    wait(pool, s_y, 16 * (b + 1))
                    step(pool.tensor_tensor(y[:, :, :], y[:, :, :],
                                            bo_row[:, :].unsqueeze(1).to_broadcast([P, KC, D]), ALU.add))
                elif name == "norm_o":
                    b, = args
                    for i in range(2):
                        wait(pool, s_oraw[i], 16 * 2 * UPB * (b + 1))
                    wait(pool, s_den, 16 * (2 + H) * (b + 1))
                    for c in range(DC):
                        o = o_feat[b % 2][:, c, :]
                        step(pool.tensor_tensor(o, o, o_den[:, c, :], ALU.mult))
                        step(pool.tensor_scalar(o, o, bias[:, 2, c:c + 1], None, ALU.add))

        @block.scalar
        def _(act):
            def drain(n, name, args):
                if name not in ("Q", "K", "V", "T", "M"):
                    return
                wait(act, s_fill, n + 1)
                if name in ("Q", "K"):
                    b, c, half = args
                    which = "QK".index(name)
                    if n < 8:
                        wait(act, s_par, 16 * 9)
                    if half == 0 and (b, c) != (0, 0):
                        pb, pc = divmod(b * DC + c - 1, DC)
                        wait(act, s_pool, pool_done("split", pb, pc))
                    act.activation(feat[which][:, half * HALF:(half + 1) * HALF], ps_j[:, :], ACT.Identity,
                                   bias=bias[:, which, c:c + 1]).then_inc(s_drain, 1)
                elif name == "V":
                    b, i = args
                    wait(act, s_pv, SPB * (b - 1))
                    act.activation(v_sb[b % 2][:, 2 * i * D:(2 * i + 2) * D, 0], ps_j[:, :],
                                   ACT.Copy).then_inc(s_drain, 1)
                elif name == "T":
                    b, i = args
                    act.activation(x1_t[i % 2][:, :, :, :], ps_j[:, :].rearrange("p (a b c) -> p a b c", a=2, b=DC),
                                   ACT.Copy).then_inc(s_drain, 1)
                else:
                    u, = args
                    wait(act, s_mrow, 16 * NPART * u)
                    act.activation(max_rows[:, :], ps_j[:, :].bitcast(BF16)[0:NPART * G * KC, 0:P],
                                   ACT.Copy).then_inc(s_drain, 1)

            for t in range(first, steps_end):
                if 0 <= t < n_steps:
                    for pair in range(2):
                        wait(act, s_score, 2 * t + pair + 1)
                        wait(act, s_pv, t - 1)
                        act.activation(probs[t % 2][:, 2 * pair:2 * pair + 2, :], ps_b[pair][:, :, :], ACT.Exp,
                                       scale=float(DH) ** -0.5).then_inc(s_exp, 1)
                if 1 <= t <= n_steps and t % KC == 0:
                    n = t // KC - 1
                    wait(act, s_pv, t)
                    wait(act, s_oraw[n % 2], 16 * 2 * (n // 2))
                    act.activation(o_raw[n % 2][:, :], ps_o[:, :], ACT.Copy).then_inc(s_ocp, 1)
                for n, name, args in at_step.get(t, []):
                    drain(n, name, args)
                for b in range(nb):
                    if t == SPB * (b + 1) + 46:
                        wait(act, s_v, vec_done("top2", b))
                        act.activation(exps[:, :], shifted[:, :], ACT.Exp).then_inc(s_eexp, 1)

        @block.tensor
        def _(pe):
            def fill(n, name, args):
                wait(pe, s_drain, n)
                if name in ("Q", "K"):
                    b, c, half = args
                    if n < 8:
                        wait(pe, s_par, 16 * 9)
                    wait(pe, s_xt, 16 * (b + 1))
                    w = w_q if name == "Q" else w_k
                    for dc in range(DC):
                        ins = pe.matmul(ps_j[:, :], w[:, dc, c * P:(c + 1) * P], x_t[:, dc, half * HALF:(half + 1) * HALF],
                                        start=dc == 0, stop=dc == DC - 1)
                elif name == "V":
                    b, i = args
                    for a in range(2):
                        tok = (2 * i + a) * P
                        for dc in range(DC):
                            ins = pe.matmul(ps_j[:, a * D:(a + 1) * D], x_t[:, dc, tok:tok + P], w_v[:, dc, :],
                                            start=dc == 0, stop=dc == DC - 1)
                elif name == "M":
                    u, = args
                    wait(pe, s_v, vec_done("max_parts", u))
                    ins = pe.transpose(ps_j[:, :].bitcast(BF16)[0:NPART * G * KC, 0:P],
                                       max_parts[:, :, :].rearrange("p a b -> p (a b)"), ident_bf[:, :])
                elif name == "O":
                    b, i = args
                    wait(pe, s_pool, pool_done("norm_o", b))
                    for a in range(2):
                        tok = (2 * i + a) * P
                        for c in range(DC):
                            ins = pe.matmul(ps_j[:, a * D:(a + 1) * D], o_feat[b % 2][:, c, tok:tok + P], w_o[:, c, :],
                                            start=c == 0, stop=c == DC - 1)
                elif name == "T":
                    b, i = args
                    wait(pe, s_v, vec_done("norm", b))
                    for a in range(2):
                        for dc in range(DC):
                            at = (a * DC + dc) * P
                            ins = pe.transpose(ps_j[:, at:at + P], y[:, 2 * i + a, dc * P:(dc + 1) * P], con("ident"))
                elif name == "L":
                    b, i = args
                    for a in range(2):
                        for dc in range(DC):
                            ins = pe.matmul(ps_j[:, a * NG * NE:(a + 1) * NG * NE], x1_t[i % 2][:, a, dc, :],
                                            router[:, dc, :], start=dc == 0, stop=dc == DC - 1)
                else:
                    b, = args
                    wait(pe, s_v, vec_done("route", b))
                    lhs = ones_bf if name == "S" else tri_bf
                    for kk in range(TOPK):
                        ins = pe.matmul(ps_j[:, :], lhs[:, :], hot[kk][:, :, :, :].rearrange("p g t e -> p (g t e)"),
                                        start=kk == 0, stop=kk == TOPK - 1)
                ins.then_inc(s_fill, 1)

            def pv(t):
                u, s = divmod(t, STEPS)
                b, g = divmod(u, UPB)
                kc = s % KC
                wait(pe, s_exp, 2 * t + 2)
                if t % SPB == 0:
                    wait(pe, s_drain, job_no[("V", (b, KC // 2 - 1))] + 1)
                if kc == 0:
                    wait(pe, s_ocp, t // KC)
                v = v_sb[b % 2]
                for j in range(G):
                    at = kc * D + (g * G + j) * DH
                    ins = pe.matmul(ps_o[32 * j:32 * j + 32, :], v[:, at:at + DH, :].rearrange("p d s -> p (d s)"), probs[t % 2][:, j, :],
                                    start=kc == 0, stop=kc == KC - 1)
                ins.then_inc(s_pv, 1)

            def pass_a(ta, fills):
                u, i = divmod(ta, STEPS)
                if i == 0 and fills[0] == 0:
                    wait(pe, s_stack[u % NSTK], 16 * STACK_DMAS * (u // NSTK + 1))
                for f in fills:
                    fa = 4 * ta + f
                    hq = 2 * i + f // 2
                    j, qt, kh = hq // KC, hq % KC, f % 2
                    wait(pe, s_amax, fa - 1)
                    pe.matmul(ps_a[fa % 2][:, :], q_stack[u % NSTK][0:ROWS, j, qt * P:(qt + 1) * P],
                              k_stack[u % NSTK][0:ROWS, j, kh * HALF:(kh + 1) * HALF],
                              start=True, stop=True).then_inc(s_a, 1)

            wait(pe, s_ones, NSTK + 3)
            wait(pe, s_set, 3)
            for t in range(first, steps_end):
                ta = t + LEAD
                in_a = 0 <= ta < n_steps
                if 0 <= t < n_steps:
                    u, s = divmod(t, STEPS)
                    if s == 0:
                        wait(pe, s_mrow, 16 * NPART * (u + 1))
                    qh, kc = divmod(s, KC)
                    for pair in range(2):
                        if in_a:
                            pass_a(ta, (pair,))
                        wait(pe, s_exp, 2 * (t - 1) + pair + 1)
                        for jj in range(2):
                            j = 2 * pair + jj
                            ins = pe.matmul(ps_b[pair][:, jj, :], k_stack[u % NSTK][0:XROWS, j, kc * P:(kc + 1) * P],
                                            q_stack[u % NSTK][0:XROWS, j, qh * HALF:(qh + 1) * HALF],
                                            start=True, stop=True)
                        ins.then_inc(s_score, 1)
                elif in_a:
                    pass_a(ta, (0, 1))
                if in_a:
                    pass_a(ta, (2,))
                if 1 <= t <= n_steps:
                    pv(t - 1)
                if in_a:
                    pass_a(ta, (3,))
                for n, name, args in at_step.get(t, []):
                    fill(n, name, args)

        @block.vector
        def _(vec):
            done = [0]

            def drain(n, name, args):
                if name not in ("O", "L", "S", "R"):
                    return
                wait(vec, s_fill, n + 1)
                if name == "O":
                    b, i = args
                    wait(vec, s_pool, pool_done("bias_y", b))
                    yy = y[:, 2 * i:2 * i + 2, :]
                    vec.tensor_tensor(yy, ps_j[:, :].rearrange("p (a d) -> p a d", a=2), yy, ALU.add).then_inc(s_drain, 1)
                elif name == "L":
                    b, i = args
                    vec.tensor_copy(logits[:, 4 * i:4 * i + 4, :],
                                    ps_j[:, 0:2 * NG * NE].rearrange("p (a e) -> p a e", e=NE)).then_inc(s_drain, 1)
                elif name == "S":
                    vec.tensor_copy(totals[:, :].rearrange("p (g e t) -> p g t e", g=NG, t=KC),
                                    ps_j[:, :].rearrange("p (g t e) -> p g t e", g=NG, t=KC)).then_inc(s_drain, 1)
                else:
                    vec.tensor_copy(rank_of[:, :], ps_j[:, :]).then_inc(s_drain, 1)

            def ops_of(name, args):
                ops = []
                add = lambda emit, after=True: ops.append((emit, after))
                op = lambda after, call, *a, **kw: add(lambda: call(*a, **kw), after)
                if name == "max_parts":
                    u, = args

                    def first_op():
                        wait(vec, s_amax, 4 * STEPS * (u + 1))
                        if u:
                            wait(vec, s_fill, job_no[("M", (u - 1,))] + 1)
                        return vec.tensor_reduce(neg_max[:, :], maxima[u % 2][:, :, :], AX.X, ALU.max, negate=True)
                    add(first_op, False)
                    op(True, vec.tensor_copy, max_parts[:, 0, :], neg_max[:, :])
                    op(True, vec.tensor_tensor, max_rest[:, :], neg_max[:, :], max_parts[:, 0, :], ALU.subtract)
                    op(True, vec.tensor_copy, max_parts[:, 1, :], max_rest[:, :])
                    op(True, vec.tensor_tensor, max_parts[:, 2, :], max_rest[:, :], max_parts[:, 1, :], ALU.subtract)
                elif name == "recip":
                    b, = args

                    def first_op():
                        wait(vec, s_den, 16 * ((2 + H) * b + 1))
                        return vec.reciprocal(den[:, :], den[:, :])
                    add(first_op, False)
                elif name == "norm":
                    b, = args

                    def first_op():
                        wait(vec, s_drain, job_no[("O", (b, KC // 2 - 1))] + 1)
                        return vec.bn_stats(stats[:, 0, :], y[:, 0, :])
                    add(first_op, False)
                    for i in range(1, KC):
                        op(False, vec.bn_stats, stats[:, i, :], y[:, i, :])
                    for i in range(KC):
                        op(True, vec.bn_aggr, mean_var[:, i, :], stats[:, i, :])
                    inverse_root(vec, op, mean_var[:, :, 1], rstd, half_var, newton)
                    for i in range(KC):
                        op(True, vec.tensor_scalar, y[:, i, :], y[:, i, :], mean_var[:, i, 0:1], rstd[:, i:i + 1],
                           ALU.subtract, ALU.mult)
                elif name == "top2":
                    b, = args
                    n = KC * NG

                    def first_op():
                        wait(vec, s_drain, job_no[("L", (b, KC // 2 - 1))] + 1)
                        return vec.max(top_val[:, 0, :], logits[:, 0, :])
                    add(first_op, False)
                    for i in range(1, n):
                        op(False, vec.max, top_val[:, i, :], logits[:, i, :])
                    op(True, vec.tensor_tensor, shifted[:, 0:n * NE].rearrange("p (a e) -> p a e", e=NE), logits[:, :, :],
                       top_val[:, :, 0:1].to_broadcast([P, n, NE]), ALU.subtract)
                    op(False, vec.tensor_tensor, shifted[:, n * NE:], top_val[:, :, 1], top_val[:, :, 0], ALU.subtract)
                    for i in range(n):
                        op(False, vec.max_index, top_idx[:, i, :], top_val[:, i, :], logits[:, i, :])
                elif name == "route":
                    b, = args
                    n = KC * NG
                    tile = slice(b * KC, (b + 1) * KC)
                    by = lambda x: x.rearrange("p (t g) -> p g t", g=NG)

                    def first_op():
                        wait(vec, s_eexp, b + 1)
                        return vec.tensor_reduce(denom[:, :], exps[:, 0:n * NE].rearrange("p (a e) -> p a e", e=NE), AX.X, ALU.add)
                    add(first_op, False)
                    op(True, vec.reciprocal, denom[:, :], denom[:, :])
                    op(True, vec.tensor_scalar, keep["weight"][:, 0, :, tile], by(denom[:, :]), 0.5, None, ALU.mult)
                    op(True, vec.tensor_tensor, keep["weight"][:, 1, :, tile], by(exps[:, n * NE:]),
                       keep["weight"][:, 0, :, tile], ALU.mult)
                    for kk in range(TOPK):
                        op(False, vec.tensor_copy, keep["expert"][:, kk, :, tile], by(top_idx[:, :, kk]))
                    for kk in range(TOPK):
                        op(True, vec.tensor_tensor, hot[kk][:, :, :, :],
                           con("iota")[:, 0:NE].unsqueeze(1).unsqueeze(1).to_broadcast([P, NG, KC, NE]),
                           keep["expert"][:, kk, :, tile].unsqueeze(3).to_broadcast([P, NG, KC, NE]), ALU.is_equal)
                elif name == "ranks":
                    b, = args
                    tile = slice(b * KC, (b + 1) * KC)
                    get = lambda x: x.rearrange("p (g e t) -> p g e t", g=NG, t=KC)

                    def first_op():
                        wait(vec, s_drain, job_no[("R", (b,))] + 1)
                        return vec.tensor_tensor_scan(incl[:, :], con("scan"), totals[:, :], 0.0, ALU.mult, ALU.add)
                    add(first_op, False)
                    op(True, vec.tensor_tensor, totals[:, :], incl[:, :], totals[:, :], ALU.subtract)
                    op(True, vec.tensor_tensor, get(totals[:, :]), get(totals[:, :]),
                       keep["count"][:, :, :].unsqueeze(3).to_broadcast([P, NG, NE, KC]), ALU.add)
                    op(True, vec.tensor_tensor, keep["count"][:, :, :], keep["count"][:, :, :],
                       get(incl[:, :])[:, :, :, KC - 1], ALU.add)
                    rr = rank_of[:, :].rearrange("p (g t e) -> p g t e", g=NG, t=KC)
                    ii = incl[:, :].rearrange("p (g t e) -> p g t e", g=NG, t=KC)
                    op(True, vec.tensor_tensor, rr, rr, get(totals[:, :]).rearrange("p g e t -> p g t e"), ALU.add)
                    op(True, vec.tensor_tensor, ii, rr, hot[0][:, :, :, :], ALU.mult)
                    op(True, vec.tensor_tensor, rr, rr, hot[1][:, :, :, :], ALU.mult)
                    op(True, vec.tensor_reduce, keep["rank"][:, 0, :, tile], ii, AX.X, ALU.add)
                    op(False, vec.tensor_reduce, keep["rank"][:, 1, :, tile], rr, AX.X, ALU.add)
                assert len(ops) == VEC_STEPS[name], (name, len(ops))
                return ops

            open_tasks, last_op = {}, {}

            def deal(t, slot):
                for name, args, i in vec_deal.get((t, slot), []):
                    key = (name, args)
                    if i == 0:
                        open_tasks[key] = ops_of(name, args)
                    emit, after = open_tasks[key][i]
                    if after:
                        wait(vec, s_v, last_op[key])
                    emit().then_inc(s_v, 1)
                    done[0] += 1
                    last_op[key] = done[0]

            vec.wait_ge(s_par, 16 * 9)
            vec.memset(keep["count"][:, :, :], 0.0).then_inc(s_set, 1)
            vec.tensor_copy(ident_bf[:, :], con("ident")).then_inc(s_set, 1)
            vec.tensor_copy(tri_bf[:, :], con("tri")).then_inc(s_set, 1)
            wait(vec, s_set, 3)
            for t in range(first, steps_end):
                ta = t + LEAD
                if 0 <= ta < n_steps:
                    u, i = divmod(ta, STEPS)
                    if i == 0 and u >= 2:
                        wait(vec, s_v, vec_done("max_parts", u - 2))
                    for f in range(4):
                        fa = 4 * ta + f
                        hq = 2 * i + f // 2
                        wait(vec, s_a, fa + 1)
                        vec.tensor_reduce(maxima[u % 2][:, hq, f % 2:f % 2 + 1], ps_a[fa % 2][:, :], AX.X,
                                          ALU.max).then_inc(s_amax, 1)
                        deal(t, f)
                else:
                    for slot in range(4):
                        deal(t, slot)
                for n, name, args in at_step.get(t, []):
                    drain(n, name, args)


def inverse_root(vec, op, var, rstd, half_var, scratch):
    op(True, vec.tensor_scalar, half_var[:, :], var, EPS, None, ALU.add)
    op(True, vec.tensor_scalar, rstd[:, :].bitcast(I32), half_var[:, :].bitcast(I32), 1, None, ALU.arith_shift_right)
    op(True, vec.tensor_scalar, rstd[:, :].bitcast(I32), rstd[:, :].bitcast(I32), -1.0, float(RSQRT_SEED), ALU.mult, ALU.add)
    for _ in range(3):
        op(True, vec.tensor_tensor, scratch[:, :], rstd[:, :], rstd[:, :], ALU.mult)
        op(True, vec.scalar_tensor_tensor, scratch[:, :], scratch[:, :], -0.5, half_var[:, :], ALU.mult, ALU.mult)
        op(True, vec.scalar_tensor_tensor, rstd[:, :], scratch[:, :], 1.5, rstd[:, :], ALU.add, ALU.mult)


def tables(tiles):
    cols, width = const_layout(tiles)
    out = np.zeros((P, width), np.float32)
    trig = np.zeros((P, 2, L), np.float32)
    put = lambda name, v: out.__setitem__((slice(None), slice(cols[name][0], cols[name][0] + cols[name][1])), v)
    inv_freq = (np.float32(1.0) / np.float32(10000.0) ** (np.arange(0, DH, 2, dtype=np.float32) / np.float32(DH))).astype(np.float32)
    angle = (np.arange(L, dtype=np.float32)[:, None] * inv_freq[None, :]).astype(np.float32).T
    dim = np.arange(P) // (P // DH)
    trig[:, 0] = np.cos(angle)[dim % (DH // 2)]
    trig[:, 1] = (np.sin(angle)[dim % (DH // 2)] * np.where(dim < DH // 2, np.float32(-1), np.float32(1))[:, None])
    put("ident", np.eye(P, dtype=np.float32))
    put("tri", np.triu(np.ones((P, P), np.float32), 1))
    put("iota", np.arange(cols["iota"][1], dtype=np.float32)[None, :])
    put("scan", (np.arange(NG * NE * KC) % KC != 0).astype(np.float32)[None, :])
    put("pid", np.arange(P, dtype=np.float32)[:, None])
    return out, trig


def host_arrays(inp, nb):
    x = np.ascontiguousarray(inp["attn_x"][:nb])
    by_dim = np.arange(D).reshape(DC, P // DH, DH).transpose(0, 2, 1).reshape(D)
    chunks = lambda w: np.ascontiguousarray(w.reshape(DC, P, -1).transpose(1, 0, 2))
    out = {
        "x_t": np.ascontiguousarray(x.transpose(0, 2, 1).reshape(nb, DC, P, L).transpose(0, 2, 1, 3)),
        "x": np.ascontiguousarray(x.reshape(nb, KC, P, D).transpose(0, 2, 1, 3)),
        "w_q": chunks(inp["attn_Wq"].T[:, by_dim]),
        "w_k": chunks(inp["attn_Wk"].T[:, by_dim]),
        "w_v": chunks(inp["attn_Wv"].T),
        "w_o": chunks(inp["attn_Wo"].T),
        "bias": np.ascontiguousarray(np.stack([inp["attn_bq"][by_dim], inp["attn_bk"][by_dim], inp["attn_bv"]])
                                     .reshape(3, DC, P).transpose(2, 0, 1)),
        "bo_row": np.ascontiguousarray(np.broadcast_to(inp["attn_bo"][None, :], (P, D))),
        "router": chunks(np.concatenate([inp["ffn_router_w0"], inp["ffn_router_w1"]], axis=1)),
    }
    out["consts"], out["trig"] = tables(n_tiles(nb * L))
    by_chunk = lambda w: w.reshape(NE, DC, P, HID).transpose(2, 0, 1, 3)
    for g in range(NG):
        out[f"w_gu{g}"] = np.ascontiguousarray(np.stack([by_chunk(inp[f"ffn_wg{g}"]), by_chunk(inp[f"ffn_wu{g}"])], axis=3))
        out[f"w_d{g}"] = np.ascontiguousarray(inp[f"ffn_wd{g}"].transpose(1, 0, 2))
    return out



def expert_phase(nc, nb, dram, keep, cols):
    tokens = nb * L
    NT = n_tiles(tokens)
    TT = nb * KC
    N = NG * NT
    NXG, NXT, NY, NC, NHOT = 4, 3, 3, 6, 8
    PAIRS = TOPK * TT
    OWNER_STEPS = 12
    START = 2

    def pairs_at(n):
        span = NT - 12 - START
        part = lambda i: min(PAIRS, max(0, i) * PAIRS // span)
        return range(part(n - START), part(n - START + 1))

    def adds_at(n, lag):
        span = NT - 12 - lag
        part = lambda i: min(PAIRS, max(0, i) * PAIRS // span)
        return range(part(n - NT - lag), part(n - NT - lag + 1))

    with ExitStack() as ctx:
        sb = lambda name, shape, dt=F32: ctx.enter_context(nc.sbuf_tensor(name + "_sb", shape, dt))
        ps = lambda name, shape: ctx.enter_context(nc.psum_tensor(name, shape, F32))
        sem = lambda name: ctx.enter_context(nc.semaphore(name))
        consts = keep["consts"]
        con = lambda name: consts[:, cols[name][0]:cols[name][0] + cols[name][1]]

        w_gu = [sb(f"w_gu{g}", [P, NE * DC * 2 * HID]) for g in range(NG)]
        w_d = sb("w_d", [P, NE * D])
        acc = w_gu[0][:, 0:TT * D].rearrange("p (t d) -> p t d", d=D)
        x_rows = [sb(f"x_rows{i}", [P, D]) for i in range(NXG)]
        x_cols = [sb(f"x_cols{i}", [P, DC, P]) for i in range(NXT)]
        gate = [sb(f"gate{i}", [P, HID]) for i in range(2)]
        hidden = [sb(f"hidden{i}", [P, HID]) for i in range(2)]
        hidden_t = [sb(f"hidden_t{i}", [P, P]) for i in range(2)]
        y_rows = [sb(f"y_rows{i}", [P, D]) for i in range(NY)]
        back = [sb(f"back{i}", [P, D]) for i in range(NC)]
        n_int = sb("n_int", [P, NG, NE], I32)
        n_fl, ends, ones_ne, base = (sb(n, [P, NG, NE]) for n in ("n_fl", "ends", "ones_ne", "base"))
        tile_id, owner = sb("tile_id", [P, 2]), sb("owner", [P, 2 * NG])
        below = sb("below", [P, 2, NG, NE])
        owner_row = sb("owner_row", [2 * NG, P], I32)
        SPLIT = 2 if TT % 2 == 0 else 1
        full = sb("full", [P, TT // SPLIT, NE])
        pos_f = sb("pos_f", [P, TOPK, TT])
        pos = sb("pos", [P, TOPK, NG, TT], I32)
        part_i = sb("part_i", [P, 2, TOPK, TT], I32)
        part_f = sb("part_f", [P, 2, TOPK, TT])
        iota_bf = sb("iota_bf", [P, max(NT, P)], BF16)
        hot_place = [sb(f"hot_place{i}", [P, P], BF16) for i in range(NHOT)]
        hot_tile = [sb(f"hot_tile{i}", [P, 2, NT], BF16) for i in range(NHOT)]
        low_id = sb("low_id", [P, NT])
        ids = [sb(f"ids{g}", [P, NT], I32) for g in range(NG)]
        stats, mean_var = sb("stats2", [P, KC, 6]), sb("mean_var2", [P, KC, 2])
        rstd, half_var, newton, shift = (sb(n, [P, KC]) for n in ("rstd2", "half_var2", "newton2", "shift"))

        ps_x = [ps(f"ps_x{i}", [P, 2 * DC, P]) for i in range(2)]
        ps_g = [ps(f"ps_g{i}", [P, 512]) for i in range(2)]
        ps_h = ps("ps_h", [P, 512])
        ps_y = [ps(f"ps_y{i}", [P, 512]) for i in range(2)]
        ps_id = ps("ps_id", [P, 512])

        s_wgu = [sem(f"w_gu_in{g}") for g in range(NG)]
        s_wd = [sem(f"w_d_in{g}") for g in range(NG)]
        s_route, s_mask, s_pair = sem("routing_step"), sem("mask_made"), sem("mask_used")
        s_tab, s_owner, s_ids = sem("owners_transposed"), sem("owners_ready"), sem("ids_step")
        s_gx = [sem(f"x_rows_in{i}") for i in range(NXG)]
        s_xt, s_xc = sem("x_transposed"), sem("x_cols_made")
        s_gu, s_silu, s_hid = sem("gate_up_done"), sem("gate_made"), sem("hidden_made")
        s_ht, s_htc, s_down, s_yr = sem("hidden_transposed"), sem("hidden_t_made"), sem("down_done"), sem("y_rows_made")
        s_yout = [sem(f"y_out{i}") for i in range(NY)]
        s_acc = sem("acc_in")
        s_back = [sem(f"back_in{i}") for i in range(NC)]
        s_add = sem("row_added")
        s_norm, s_fin, s_out = sem("norm_step"), sem("normalised"), sem("out_written")
        block = ctx.enter_context(nc.Block())

        def wait(eng, s, value):
            if value > 0:
                eng.wait_ge(s, value)

        WCHUNK = 4
        def load_weights(sp, g):
            for i in range(WCHUNK):
                n = NE // WCHUNK
                w = DC * 2 * HID
                sp.dma_start(w_gu[g][:, i * n * w:(i + 1) * n * w],
                             dram[f"w_gu{g}"][:, i * n:(i + 1) * n].rearrange("p e c s h -> p (e c s h)")).then_inc(s_wgu[g], 16)

        def load_down(sp, g):
            sp.dma_start(w_d[:, :], dram[f"w_d{g}"].rearrange("p e d -> p (e d)")).then_inc(s_wd[g], 16)

        def store_y(sp, n):
            g, i = divmod(n, NT)
            wait(sp, s_yr, n + 1)
            sp.dma_start(dram["y"][g][i * P:(i + 1) * P, :], y_rows[n % NY][:, :]).then_inc(s_yout[n % NY], 16)

        def stored(eng, tiles):
            for i in range(NY):
                wait(eng, s_yout[i], 16 * len(range(i, tiles, NY)))

        NORM = KC + KC + 3 + 9 + 1
        adds = [(g, t, kk) for g in range(NG) for t in range(TT) for kk in range(TOPK)]

        @block.sync
        def _(sp):
            load_weights(sp, 0)
            load_down(sp, 0)
            load_weights(sp, 1)
            for n in range(N):
                store_y(sp, n)
                if n == NT - 1:
                    wait(sp, s_down, NT)
                    load_down(sp, 1)
                    wait(sp, s_gu, NT)
                    for b in range(nb):
                        sp.dma_start(acc[:, b * KC:(b + 1) * KC, :],
                                     dram["x1"][b * L:(b + 1) * L, :].rearrange("(t p) d -> p t d", p=P)).then_inc(s_acc, 16)
            for b in range(nb):
                wait(sp, s_fin, KC * (b + 1))
                sp.dma_start(dram["out"][b].rearrange("(t p) d -> p t d", p=P),
                             acc[:, b * KC:(b + 1) * KC, :]).then_inc(s_out, 16)
            sp.wait_ge(s_out, 16 * nb)

        @block.gpsimd
        def _(pool):
            def gather(n):
                g, i = divmod(n, NT)
                if i == 0:
                    wait(pool, s_ids, 2 * (g + 1))
                wait(pool, s_xt, n - NXG + 1)
                pool.indirect_dma_start(x_rows[n % NXG][:, :], None, dram["x1"][:, :],
                                        bass.IndirectOffsetOnAxis(ap=ids[g][:, i:i + 1], axis=0)).then_inc(s_gx[n % NXG], 16)

            def fetch(a):
                g, t, kk = adds[a]
                if t == 0 and kk == 0:
                    stored(pool, NT * (g + 1))
                wait(pool, s_add, a - NC + 1)
                pool.indirect_dma_start(back[a % NC][:, :], None, dram["y"][g],
                                        bass.IndirectOffsetOnAxis(ap=pos[:, kk, g, t:t + 1], axis=0)).then_inc(s_back[a % NC], 16)

            for n in range(NT):
                gather(n)
            for n in range(NT, N):
                gather(n)
                for a in adds_at(n, 8):
                    fetch(a)
            for a in range(PAIRS, len(adds)):
                fetch(a)

        @block.scalar
        def _(act):
            def columns(n):
                wait(act, s_xt, n + 1)
                wait(act, s_gu, n - NXT + 1)
                act.activation(x_cols[n % NXT][:, :, :], ps_x[n % 2][:, 0:DC, :], ACT.Copy).then_inc(s_xc, 1)

            for n in range(-1, N):
                if n >= 0:
                    wait(act, s_gu, n + 1)
                    wait(act, s_hid, n - 1)
                    act.activation(gate[n % 2][:, :], ps_g[n % 2][:, 0:HID], ACT.Silu).then_inc(s_silu, 1)
                for m in ((0, 1) if n == -1 else (n + 2,)):
                    if m < N:
                        columns(m)
            for b in range(nb):
                wait(act, s_norm, NORM * (b + 1))
                for i in range(KC):
                    t = b * KC + i
                    act.activation(acc[:, t, :], acc[:, t, :], ACT.Identity, bias=shift[:, i:i + 1],
                                   scale=rstd[:, i:i + 1]).then_inc(s_fin, 1)

        @block.tensor
        def _(pe):
            def owners():
                wait(pe, s_route, OWNER_STEPS)
                pe.transpose(ps_id[0:2 * NG, 0:P], owner[:, :], con("ident")).then_inc(s_tab, 1)

            def pair(g, m):
                n = g * PAIRS + m
                wait(pe, s_mask, n + 1)
                if m == 0:
                    wait(pe, s_owner, 1)
                    wait(pe, s_ids, 2 * g)
                pe.matmul(ps_id[:, 0:2 * NT], hot_place[n % NHOT][:, :],
                          hot_tile[n % NHOT][:, :, :].rearrange("p a t -> p (a t)"),
                          start=m == 0, stop=m == PAIRS - 1).then_inc(s_pair, 1)

            def transpose_x(n):
                wait(pe, s_gx[n % NXG], 16 * (n // NXG + 1))
                wait(pe, s_xc, n - 1)
                for dc in range(DC):
                    ins = pe.transpose(ps_x[n % 2][:, dc, :], x_rows[n % NXG][:, dc * P:(dc + 1) * P], con("ident"))
                ins.then_inc(s_xt, 1)

            def gate_up(n, e):
                g, i = divmod(n, NT)
                if i == 0:
                    wait(pe, s_wgu[g], 16 * WCHUNK)
                wait(pe, s_xc, n + 1)
                wait(pe, s_hid, n - 1)
                for dc in range(DC):
                    ins = pe.matmul(ps_g[n % 2][:, 0:2 * HID], x_cols[n % NXT][:, dc, :],
                                    w_gu[g][:, bass.ds(e * (DC * 2 * HID) + dc * 2 * HID, 2 * HID)],
                                    start=dc == 0, stop=dc == DC - 1)
                ins.then_inc(s_gu, 1)

            def transpose_h(n):
                wait(pe, s_hid, n + 1)
                wait(pe, s_htc, n)
                pe.transpose(ps_h[:, 0:P], hidden[n % 2][:, :], con("ident")).then_inc(s_ht, 1)

            def down(n, e):
                g, i = divmod(n, NT)
                if i == 0:
                    wait(pe, s_wd[g], 16)
                wait(pe, s_htc, n + 1)
                wait(pe, s_yr, n - 1)
                pe.matmul(ps_y[n % 2][:, 0:D], hidden_t[n % 2][:, :], w_d[:, bass.ds(e * D, D)],
                          start=True, stop=True).then_inc(s_down, 1)

            owners()
            for m in range(PAIRS):
                pair(0, m)
            wait(pe, s_owner, 1)
            expert = {}
            for n in range(N + 2):
                if n == 0:
                    transpose_x(0)
                    transpose_x(1)
                if n < N:
                    g, i = divmod(n, NT)
                    row = (i // P) * NG + g
                    expert[n] = pe.value_load(owner_row[row:row + 1, i % P:i % P + 1], min_val=0, max_val=NE - 1)
                    gate_up(n, expert[n])
                if 1 <= n <= N:
                    transpose_h(n - 1)
                if 2 <= n:
                    down(n - 2, expert.pop(n - 2))
                if n + 2 < N:
                    transpose_x(n + 2)
                for m in pairs_at(n - 2):
                    pair(1, m)

        @block.vector
        def _(vec):
            done = [0]

            def step(ins, chained=True):
                ins.then_inc(s_route, 1)
                done[0] += 1
                if chained:
                    vec.wait_ge(s_route, done[0])

            def positions(g):
                n = TT // SPLIT
                for kk in range(TOPK):
                    for i in range(SPLIT):
                        tiles = slice(i * n, (i + 1) * n)
                        step(vec.tensor_tensor(full[:, :, :], con("iota")[:, 0:NE].unsqueeze(1).to_broadcast([P, n, NE]),
                                               keep["expert"][:, kk, g, tiles].unsqueeze(2).to_broadcast([P, n, NE]), ALU.is_equal))
                        step(vec.tensor_tensor(full[:, :, :], full[:, :, :],
                                               base[:, g, :].unsqueeze(1).to_broadcast([P, n, NE]), ALU.mult))
                        step(vec.tensor_reduce(pos_f[:, kk, tiles], full[:, :, :], AX.X, ALU.add))
                step(vec.tensor_tensor(pos_f[:, :, :], pos_f[:, :, :], keep["rank"][:, :, g, :], ALU.add))
                step(vec.tensor_copy(pos[:, :, g, :], pos_f[:, :, :]))
                step(vec.tensor_scalar(part_i[:, 0], pos[:, :, g, :], P - 1, None, ALU.bitwise_and), chained=False)
                step(vec.tensor_scalar(part_i[:, 1], pos[:, :, g, :], 7, None, ALU.arith_shift_right))
                step(vec.tensor_copy(part_f[:, :, :, :], part_i[:, :, :, :]))

            def mask(g, m):
                n = g * PAIRS + m
                kk, t = divmod(m, TT)
                wait(vec, s_pair, n - NHOT + 1)
                place, tile = part_f[:, 0, kk, t:t + 1], part_f[:, 1, kk, t:t + 1]
                vec.tensor_scalar(hot_place[n % NHOT][:, :], iota_bf[:, 0:P], place, None, ALU.is_equal)
                vec.tensor_scalar(hot_tile[n % NHOT][:, 0, :], iota_bf[:, 0:NT], tile, con("pid"), ALU.is_equal, ALU.mult)
                vec.tensor_scalar(hot_tile[n % NHOT][:, 1, :], iota_bf[:, 0:NT], tile, float(t), ALU.is_equal,
                                  ALU.mult).then_inc(s_mask, 1)

            def read_ids(g):
                wait(vec, s_pair, (g + 1) * PAIRS)
                vec.tensor_copy(low_id[:, :], ps_id[:, 0:NT]).then_inc(s_ids, 1)
                vec.wait_ge(s_ids, 2 * g + 1)
                vec.scalar_tensor_tensor(ids[g][:, :], ps_id[:, NT:2 * NT], float(P), low_id[:, :], ALU.mult,
                                         ALU.add).then_inc(s_ids, 1)

            step(vec.memset(ones_ne[:, :, :], 1.0), chained=False)
            step(vec.tensor_scalar(n_int[:, :, :], keep["count"][:, :, :], float(P - 1), None, ALU.add))
            step(vec.tensor_scalar(n_int[:, :, :], n_int[:, :, :], 7, None, ALU.arith_shift_right))
            step(vec.tensor_copy(n_fl[:, :, :], n_int[:, :, :]))
            for g in range(NG):
                ins = vec.tensor_tensor_scan(ends[:, g, :], ones_ne[:, g, :], n_fl[:, g, :], 0.0, ALU.mult, ALU.add)
                step(ins, chained=g == NG - 1)
            for hi in range(2):
                step(vec.tensor_scalar(tile_id[:, hi:hi + 1], con("pid"), float(hi * P), None, ALU.add), chained=hi == 1)
            for hi in range(2):
                step(vec.tensor_tensor(below[:, hi, :, :], ends[:, :, :],
                                       tile_id[:, hi:hi + 1].unsqueeze(2).to_broadcast([P, NG, NE]), ALU.is_le),
                     chained=hi == 1)
            step(vec.tensor_reduce(owner[:, :].rearrange("p (h g) -> p h g", h=2), below[:, :, :, :], AX.X, ALU.add))
            step(vec.tensor_scalar(owner[:, :], owner[:, :], float(NE - 1), None, ALU.min))
            assert done[0] == OWNER_STEPS
            step(vec.tensor_tensor(base[:, :, :], ends[:, :, :], n_fl[:, :, :], ALU.subtract))
            step(vec.tensor_scalar(base[:, :, :], base[:, :, :], float(P), None, ALU.mult), chained=False)
            step(vec.tensor_copy(iota_bf[:, :], con("iota")))
            wait(vec, s_tab, 1)
            vec.tensor_copy(owner_row[:, :], ps_id[0:2 * NG, 0:P]).then_inc(s_owner, 1)
            positions(0)
            for m in range(PAIRS):
                mask(0, m)
            read_ids(0)

            def tile_work(n):
                if n < N:
                    wait(vec, s_silu, n + 1)
                    wait(vec, s_ht, n - 1)
                    vec.tensor_tensor(hidden[n % 2][:, :], gate[n % 2][:, :], ps_g[n % 2][:, HID:2 * HID],
                                      ALU.mult).then_inc(s_hid, 1)
                if 1 <= n <= N:
                    m = n - 1
                    wait(vec, s_ht, m + 1)
                    wait(vec, s_down, m - 1)
                    vec.tensor_copy(hidden_t[m % 2][:, :], ps_h[:, 0:P]).then_inc(s_htc, 1)
                if 2 <= n:
                    m = n - 2
                    wait(vec, s_down, m + 1)
                    if m >= NY:
                        wait(vec, s_yout[m % NY], 16 * (m // NY))
                    vec.tensor_copy(y_rows[m % NY][:, :], ps_y[m % 2][:, 0:D]).then_inc(s_yr, 1)

            def add(a):
                g, t, kk = adds[a]
                if a == 0:
                    wait(vec, s_acc, 16 * nb)
                wait(vec, s_back[a % NC], 16 * (a // NC + 1))
                wait(vec, s_add, a)
                vec.scalar_tensor_tensor(acc[:, t, :], back[a % NC][:, :], keep["weight"][:, kk, g, t:t + 1], acc[:, t, :],
                                         ALU.mult, ALU.add).then_inc(s_add, 1)

            for n in range(N + 2):
                tile_work(n)
                if n == START - 1:
                    positions(1)
                if n < NT:
                    for m in pairs_at(n):
                        mask(1, m)
                    if n == NT - 8:
                        read_ids(1)
                for a in adds_at(n, 10):
                    add(a)
            a = PAIRS
            nd = [0]

            def nstep(ins, chained=True):
                ins.then_inc(s_norm, 1)
                nd[0] += 1
                if chained:
                    vec.wait_ge(s_norm, nd[0])

            for b in range(nb):
                if b:
                    wait(vec, s_fin, KC * b)
                for i in range(KC):
                    for _ in range(TOPK):
                        add(a)
                        a += 1
                    vec.wait_ge(s_add, a)
                    nstep(vec.bn_stats(stats[:, i, :], acc[:, b * KC + i, :]), chained=i == KC - 1)
                for i in range(KC):
                    nstep(vec.bn_aggr(mean_var[:, i, :], stats[:, i, :]), chained=i == KC - 1)
                inverse_root(vec, lambda after, call, *a: nstep(call(*a)), mean_var[:, :, 1], rstd, half_var, newton)
                nstep(vec.scalar_tensor_tensor(shift[:, :], mean_var[:, :, 0], -1.0, rstd[:, :], ALU.mult, ALU.mult))


def build(nc, nb, a, debug=False, only=None):
    tokens = nb * L
    cols, width = const_layout(n_tiles(tokens))
    with ExitStack() as ctx:
        sb = lambda name, shape, dt=F32: ctx.enter_context(nc.sbuf_tensor(name + "_sb", shape, dt))
        keep = {
            "rank": sb("rank", [P, TOPK, NG, nb * KC]),
            "expert": sb("expert", [P, TOPK, NG, nb * KC]),
            "weight": sb("weight", [P, TOPK, NG, nb * KC]),
            "count": sb("count", [P, NG, NE]),
            "consts": sb("consts", [P, width]),
        }
        dram = dict(a)
        dram["parts"] = nc.dram_tensor("parts_dram", [nb * DC, 2, NPART, P, L], BF16, kind="Internal").ap()
        dram["den"] = nc.dram_tensor("den_dram", [nb, H, L], F32, kind="Internal").ap()
        dram["inv"] = nc.dram_tensor("inv_dram", [nb, H, L], F32, kind="Internal").ap()
        dram["y"] = [nc.dram_tensor(f"y_dram{g}", [n_tiles(tokens) * P, D], F32, kind="Internal").ap() for g in range(NG)]
        if "out" in a:
            if "x1" not in a:
                dram["x1"] = nc.dram_tensor("x1_dram", [tokens, D], F32, kind="Internal").ap()
        attention_phase(nc, nb, dram, keep, {"cols": cols})
        if "out" in a:
            expert_phase(nc, nb, dram, keep, cols)
        if debug:
            with nc.semaphore("dbg") as s, nc.Block() as block:
                @block.sync
                def _(sp):
                    n = nb * KC
                    for i, name in enumerate(("rank", "expert", "weight")):
                        dst = a["dbg"][:, 256 * i:256 * i + 256].rearrange("p (k g t) -> p k g t", k=2, g=2)[:, :, :, 0:n]
                        for kk in range(2):
                            sp.dma_start(dst[:, kk], keep[name][:, kk]).then_inc(s, 16)
                    sp.wait_ge(s, 96)


def kernel(**inputs):
    import concourse.bacc as bacc
    from concourse.bass_utils import run_bass_kernel_spmd

    arrays = host_arrays({name[3:]: np.asarray(v) for name, v in inputs.items()}, 8)
    nb = arrays["x"].shape[0]
    nc = bacc.Bacc("TRN2", target_bir_lowering=False, num_devices=1)
    args = {name: nc.dram_tensor(name, v.shape, mybir.dt.from_np(v.dtype), kind="ExternalInput").ap()
            for name, v in arrays.items()}
    args["out"] = nc.dram_tensor("out", (nb, L, D), F32, kind="ExternalOutput").ap()
    build(nc, nb, args)
    return run_bass_kernel_spmd(nc, [arrays], core_ids=[0]).results[0]["out"]
```

```python
import numpy as np
import concourse.bass as bass
from concourse import mybir
from contextlib import ExitStack

F32, BF16, I32, U32 = mybir.dt.float32, mybir.dt.bfloat16, mybir.dt.int32, mybir.dt.uint32
ALU, ACT, AX = mybir.AluOpType, mybir.ActivationFunctionType, mybir.AxisListType

P = 128
L, D, H, DH = 1024, 256, 16, 16
DC = D // P
G = 4
HALF = 512
KC = L // P
UPB = H // G
STEPS = (L // HALF) * KC
SPB = UPB * STEPS
LEAD = STEPS + 6
NPART, NTERM = 3, 6
Q_PART, Q_RUNS = (0, 0, 0, 1, 1, 2), ((0, 0, 1), (1, 0, 1), (2, 0, 2), (4, 1, 2))
K_PART, K_RUNS = (0, 1, 2, 0, 1, 0), ((0, 0, 3), (3, 0, 2), (5, 0, 1))
ROWS = NTERM * DH
XROWS = ROWS + NPART
STACK_DMAS = len(Q_RUNS) + len(K_RUNS)
NSTK = 3
EPS = 1e-5
NE, HID, NG, TOPK = 32, 128, 2, 2
RSQRT_SEED = 0x5F3759DF


def n_tiles(tokens):
    return (tokens * TOPK + NE * (P - 1)) // P


def const_layout(tiles):
    at, out = 0, {}
    for name, width in (("ident", P), ("tri", P), ("iota", max(tiles, P)),
                        ("scan", NG * NE * KC), ("pid", 1)):
        out[name] = (at, width)
        at += width
    return out, at


def schedule(nb):
    jobs = []
    for b in range(nb):
        start, end = SPB * b, SPB * (b + 1)
        for i, (what, half) in enumerate((("Q", 0), ("Q", 1), ("K", 0), ("K", 1))):
            for c, at in enumerate((start - 46, start - 20)):
                jobs.append((at + 2 * i, what, (b, c, half)))
        for i in range(KC // 2):
            jobs.append((start - 8 + 2 * i, "V", (b, i)))
            jobs.append((end + (12, 13, 15, 16)[i], "O", (b, i)))
            jobs.append((end + 26 + 2 * i, "T", (b, i)))
            jobs.append((end + 27 + 2 * i, "L", (b, i)))
        for u in range(UPB):
            jobs.append((start + STEPS * u - 5, "M", (UPB * b + u,)))
        jobs.append((end + 54, "S", (b,)))
        jobs.append((end + 55, "R", (b,)))
    order = {n: i for i, n in enumerate("MQKVOTLSR")}
    jobs.sort(key=lambda j: (j[0], order[j[1]]))
    return jobs


BLANK = 4
LONG_JOBS = "QKVO"
VEC_COST = {
    "max_parts": [1] * 5,
    "recip": [6],
    "norm": [3] * KC + [1] * (KC + 3 + 9) + [3] * KC,
    "top2": [1] * KC * NG + [6, 1] + [1] * KC * NG,
    "route": [6, 1, 1, 1, 1, 1, 6, 6],
    "ranks": [6] * 9 + [1],
}


def list_tokens(pool, b, dram, keep):
    for t in range(KC):
        for kk in range(TOPK):
            pool.indirect_dma_start(dram["list"], bass.IndirectOffsetOnAxis(ap=keep["listed"][:, kk, t:t + 1], axis=0),
                                    keep["token"][:, b * KC + t:b * KC + t + 1], None).then_inc(keep["s_list"], 16)


def attention_phase(nc, nb, dram, keep, cols):
    jobs = schedule(nb)
    job_no = {(name, args): n for n, (_, name, args) in enumerate(jobs)}
    at_step = {}
    for n, (t, name, args) in enumerate(jobs):
        at_step.setdefault(t, []).append((n, name, args))
    n_steps = SPB * nb
    first, last = min(at_step), max(at_step)
    n_units = UPB * nb
    n_blank = -(-n_tiles(nb * L) // BLANK)

    with ExitStack() as ctx:
        sb = lambda name, shape, dt=F32: ctx.enter_context(nc.sbuf_tensor(name + "_sb", shape, dt))
        ps = lambda name, shape: ctx.enter_context(nc.psum_tensor(name, shape, F32))
        sem = lambda name: ctx.enter_context(nc.semaphore(name))

        x_t = sb("x_t", [P, DC, L])
        w_q, w_k, w_v, w_o = (sb(n, [P, DC, D]) for n in ("w_q", "w_k", "w_v", "w_o"))
        bias = sb("bias", [P, 3, DC])
        bo_row = sb("bo_row", [P, D])
        trig = sb("trig", [P, 2, L])
        router = sb("router", [P, DC, NG * NE])
        feat = [sb(f"feat_{n}", [P, L]) for n in "qk"]
        swapped = sb("swapped", [P, L])
        parts = [sb(f"parts_{n}", [P, NPART, L], BF16) for n in "qk"]
        q_stack = [sb(f"q_stack{i}", [P, G, L], BF16) for i in range(NSTK)]
        k_stack = [sb(f"k_stack{i}", [P, G, L], BF16) for i in range(NSTK)]
        v_sb = [sb(f"v_sb{i}", [P, KC * D, 2]) for i in range(2)]
        probs = [sb(f"probs{i}", [P, G, HALF]) for i in range(2)]
        maxima = [sb(f"maxima{i}", [P, G * KC, 2]) for i in range(2)]
        neg_max = sb("neg_max", [P, G * KC])
        max_rest = sb("max_rest", [P, G * KC])
        max_parts = sb("max_parts", [P, NPART, G * KC], BF16)
        max_rows = sb("max_rows", [NPART * G * KC, P], BF16)
        o_raw = [sb(f"o_raw{i}", [P, HALF]) for i in range(2)]
        o_feat = [sb(f"o_feat{i}", [P, DC, L]) for i in range(2)]
        o_den = sb("o_den", [P, DC, L])
        listed = keep["listed"]
        den = sb("den", [P, H * L // P])
        y = sb("y", [P, KC, D])
        stats, mean_var = sb("stats", [P, KC, 6]), sb("mean_var", [P, KC, 2])
        rstd, half_var, newton = (sb(n, [P, KC]) for n in ("rstd", "half_var", "newton"))
        x1_t = [sb(f"x1_t{i}", [P, 2, DC, P]) for i in range(2)]
        logits = sb("logits", [P, KC * NG, NE])
        top_val = sb("top_val", [P, KC * NG, 8])
        top_idx = sb("top_idx", [P, KC * NG, 8], U32)
        shifted = sb("shifted", [P, KC * NG * NE + KC * NG])
        exps = shifted
        denom = sb("denom", [P, KC * NG])
        hot = [sb(f"hot{i}", [P, NG, KC, NE], BF16) for i in range(TOPK)]
        totals, incl = (sb(n, [P, NG * NE * KC]) for n in ("totals", "incl"))
        rank_of = logits[:, :, :].rearrange("p a e -> p (a e)")
        ident_bf, tri_bf, ones_bf = (sb(n, [P, P], BF16) for n in ("ident_bf", "tri_bf", "ones_bf"))

        ps_b = [ps(f"ps_b{i}", [P, 2, HALF]) for i in range(2)]
        ps_a = [ps(f"ps_a{i}", [P, HALF]) for i in range(2)]
        ps_o = ps("ps_o", [P, HALF])
        ps_j = ps("ps_j", [P, HALF])

        s_par, s_xt, s_y = sem("parameters_in"), sem("x_t_in"), sem("y_in")
        s_set, s_ones = sem("constants_made"), sem("ones_made")
        s_fill, s_drain = sem("job_filled"), sem("job_drained")
        s_score, s_exp, s_pv = sem("scored"), sem("exponentiated"), sem("pv_done")
        s_a, s_amax = sem("a_scored"), sem("a_maximum")
        s_den = sem("den_moved")
        s_oraw = [sem(f"o_raw_out{i}") for i in range(2)]
        s_ocp = sem("o_copied")
        s_swap, s_parts = sem("swapped_in"), sem("parts_out")
        s_pool = sem("pool_step")
        s_stack = [sem(f"stack_in{i}") for i in range(NSTK)]
        s_mrow = sem("max_rows_in")
        s_v = sem("vector_step")
        s_x1 = sem("x1_out")
        s_eexp = sem("router_exp")
        s_zero, s_blank, s_cleared = sem("blank_made"), sem("blank_out"), sem("list_cleared")
        s_list = keep["s_list"]
        block = ctx.enter_context(nc.Block())

        consts = keep["consts"]
        con = lambda name: consts[:, cols[name][0]:cols[name][0] + cols[name][1]]

        pool_no = {}

        def pool_plan():
            todo = []
            for b in range(nb):
                for c in range(DC):
                    at = job_step[("K", (b, c, 1))]
                    todo.append((at, "split", (b, c)))
                todo.append((SPB * b + 40, "bias_y", (b,)))
                todo.append((SPB * (b + 1) + 4, "norm_o", (b,)))
                if b < nb - 1:
                    todo.append((SPB * (b + 2) + 10, "list", (b,)))
            todo.sort(key=lambda x: x[0])
            return todo

        job_step = {(name, args): t for t, name, args in jobs}
        todo_pool = pool_plan()
        POOL_STEPS = {"split": 14, "bias_y": 1, "norm_o": 2 * DC, "list": 0}
        count = 0
        for _, name, args in todo_pool:
            pool_no[(name, args)] = count
            count += POOL_STEPS[name]

        vec_tasks = [(STEPS * u - 6, 0, "max_parts", (u,)) for u in range(n_units)]
        for b in range(nb):
            end = SPB * (b + 1)
            vec_tasks += [(end + 3, 1, "recip", (b,)), (end + 17, 2, "norm", (b,)), (end + 34, 3, "top2", (b,)),
                          (end + 47, 4, "route", (b,)), (end + 56, 5, "ranks", (b,))]
        vec_tasks.sort()
        VEC_STEPS = {name: len(cost) for name, cost in VEC_COST.items()}
        steps_end = max(last, vec_tasks[-1][0], n_steps) + 1
        vec_deal, vec_last, vec_step = {}, {}, {}
        waiting, left, dealt = list(vec_tasks), {}, 0
        for t in range(first, steps_end):
            for slot in range(4):
                if not 0 <= t + LEAD < n_steps:
                    room = 1 << 30
                elif slot != 2:
                    room = 0
                else:
                    room = 12 if any(name in LONG_JOBS for at in (t, t - SPB) for _, name, _ in at_step.get(at, [])) else 3
                while True:
                    ready = [x for x in waiting if x[0] <= t and (room > 0 or x[1] == 0)]
                    if not ready:
                        break
                    task = min(ready, key=lambda x: (x[1] != 0, x[0]))
                    key = task[2:]
                    k_op = left.get(key, 0)
                    vec_deal.setdefault((t, slot), []).append((*key, k_op))
                    left[key] = k_op + 1
                    dealt += 1
                    room -= VEC_COST[key[0]][k_op]
                    if k_op + 1 == VEC_STEPS[key[0]]:
                        vec_last[key], vec_step[key] = dealt, t
                        waiting.remove(task)
        assert not waiting
        for t, name, args in jobs:
            before = {"M": "max_parts", "O": "recip", "T": "norm", "S": "route", "R": "route"}.get(name)
            assert before is None or vec_step[(before, args[:1])] <= t, (t, name, args)
        vec_done = lambda name, *args: vec_last[(name, args)]
        pool_done = lambda name, *args: pool_no[(name, args)] + POOL_STEPS[name]

        def wait(eng, s, value):
            if value > 0:
                eng.wait_ge(s, value)

        def split(eng, b, c, done):
            n = b * DC + c
            wait(eng, s_parts, 16 * 2 * n)
            for which in range(2):
                f, part = feat[which], parts[which]
                wait(eng, s_drain, job_no[("QK"[which], (b, c, 1))] + 1)
                wait(eng, s_swap, 16 * 2 * (2 * n + which + 1))
                for out, x0, x1, op in ((f[:, :], f[:, :], trig[:, 0, :], ALU.mult),
                                        (swapped[:, :], swapped[:, :], trig[:, 1, :], ALU.mult),
                                        (part[:, 0, :], f[:, :], swapped[:, :], ALU.add),
                                        (f[:, :], f[:, :], swapped[:, :], ALU.add),
                                        (part[:, 1, :], f[:, :], part[:, 0, :], ALU.subtract),
                                        (f[:, :], f[:, :], part[:, 0, :], ALU.subtract),
                                        (part[:, 2, :], f[:, :], part[:, 1, :], ALU.subtract)):
                    eng.tensor_tensor(out, x0, x1, op).then_inc(s_pool, 1)
                    done += 1
                    eng.wait_ge(s_pool, done)
            return done

        def norm_o(eng, b, done):
            for i in range(2):
                wait(eng, s_oraw[i], 16 * 2 * UPB * (b + 1))
            wait(eng, s_den, 16 * (2 + H) * (b + 1))
            for c in range(DC):
                o = o_feat[b % 2][:, c, :]
                for ins in (lambda: eng.tensor_tensor(o, o, o_den[:, c, :], ALU.mult),
                            lambda: eng.tensor_scalar(o, o, bias[:, 2, c:c + 1], None, ALU.add)):
                    ins().then_inc(s_pool, 1)
                    done += 1
                    eng.wait_ge(s_pool, done)
            return done

        @block.sync
        def _(sp):
            sp.dma_start(x_t[:, :, :], dram["x_t"][0]).then_inc(s_xt, 16)
            for dst, src in ((w_q, "w_q"), (bias, "bias"), (w_k, "w_k"), (consts, "consts"), (trig, "trig"), (w_v, "w_v"),
                             (w_o, "w_o"), (bo_row, "bo_row"), (router, "router")):
                sp.dma_start(dst[:], dram[src][:]).then_inc(s_par, 16)

            def swap(b, c, which):
                wait(sp, s_drain, job_no[("QK"[which], (b, c, 1))] + 1)
                if which == 1:
                    wait(sp, s_pool, pool_no[("split", (b, c))] + 4)
                elif (b, c) != (0, 0):
                    pb, pc = divmod(b * DC + c - 1, DC)
                    wait(sp, s_pool, pool_done("split", pb, pc))
                for lo, hi in ((0, P // 2), (P // 2, 0)):
                    sp.dma_start(swapped[lo:lo + P // 2, :], feat[which][hi:hi + P // 2, :]).then_inc(s_swap, 16)

            def parts_out(b, c, which):
                wait(sp, s_pool, pool_no[("split", (b, c))] + 7 * (which + 1))
                sp.dma_start(dram["parts"][b * DC + c, which].rearrange("t p l -> p t l"),
                             parts[which][:, :, :]).then_inc(s_parts, 16)

            def stack(u):
                b, g = divmod(u, UPB)
                c = g // 2
                wait(sp, s_parts, 16 * 2 * (b * DC + c + 1))
                wait(sp, s_score, 2 * STEPS * (u - NSTK + 1))
                for stk, which, runs in ((q_stack, 0, Q_RUNS), (k_stack, 1, K_RUNS)):
                    src = dram["parts"][b * DC + c, which].rearrange("t (r j) l -> (t r) j l", j=2 * G)
                    for term, part, n in runs:
                        sp.dma_start(stk[u % NSTK][term * DH:(term + n) * DH, :, :],
                                     src[part * DH:(part + n) * DH, (g % 2) * G:(g % 2 + 1) * G, :]
                                     ).then_inc(s_stack[u % NSTK], 16)

            def max_row(u):
                wait(sp, s_drain, job_no[("M", (u,))] + 1)
                for i in range(NPART):
                    sp.dma_start(q_stack[u % NSTK][ROWS + i:ROWS + i + 1, :, :].rearrange("o j (t q) -> o (j t) q", q=P),
                                 max_rows[i * G * KC:(i + 1) * G * KC, :]).then_inc(s_mrow, 16)

            def o_out(n):
                u, half = divmod(n, 2)
                b, g = divmod(u, UPB)
                wait(sp, s_ocp, n + 1)
                if n % (2 * UPB) == 0:
                    if b >= 2:
                        wait(sp, s_fill, job_no[("O", (b - 2, KC // 2 - 1))] + 1)
                lo = (g % 2) * G * DH
                sp.dma_start(o_feat[b % 2][lo:lo + G * DH, g // 2, half * HALF:(half + 1) * HALF],
                             o_raw[n % 2][0:P:2, :]).then_inc(s_oraw[n % 2], 16)
                sp.dma_start(dram["den"][b, g * G:(g + 1) * G, half * HALF:(half + 1) * HALF],
                             o_raw[n % 2][1:P:2 * DH, :]).then_inc(s_oraw[n % 2], 16)

            def den_in(b):
                for i in range(2):
                    wait(sp, s_oraw[i], 16 * 2 * UPB * (b + 1))
                if b:
                    wait(sp, s_v, vec_done("recip", b - 1))
                    wait(sp, s_den, 16 * (2 + H) * b)
                sp.dma_start(den[:, :], dram["den"][b].rearrange("h (a l) -> (h a) l", a=P // H)).then_inc(s_den, 16)

            def den_out(b):
                wait(sp, s_v, vec_done("recip", b))
                sp.dma_start(dram["inv"][b].rearrange("h (a l) -> (h a) l", a=P // H), den[:, :]).then_inc(s_den, 16)
                if b:
                    wait(sp, s_pool, pool_done("norm_o", b - 1))
                wait(sp, s_den, 16 * ((2 + H) * b + 2))
                for h in range(H):
                    lo = h % (P // DH) * DH
                    sp.dma_start(o_den[lo:lo + DH, h * DH // P, :],
                                 dram["inv"][b, h:h + 1, :].to_broadcast([DH, L])).then_inc(s_den, 16)

            def blank(i):
                tiles = dram["rows"].rearrange("(t p) w -> p t w", p=P)[:, i * BLANK:min((i + 1) * BLANK, n_tiles(nb * L)), :]
                if i == 0:
                    wait(sp, s_zero, 1)
                    sp.dma_start(dram["list"].rearrange("(p a w) o -> p a (w o)", p=P, w=D),
                                 keep["blank"][:, 0:D].bitcast(I32).unsqueeze(1).to_broadcast([P, NE * nb * L // (P * D), D])
                                 ).then_inc(s_cleared, 16)
                sp.dma_start(tiles, keep["blank"][:, :].unsqueeze(1).to_broadcast([P, tiles.shape[1], D + 2])
                             ).then_inc(s_blank, 16)

            tasks = []
            for i in range(n_blank):
                tasks.append(((i + 1) * (n_steps - 8) / (n_blank + 1) + 0.5, 9, blank, (i,)))
            for b in range(nb):
                for c in range(DC):
                    t = job_step[("K", (b, c, 1))]
                    tasks.append((t - 1, 0, swap, (b, c, 0)))
                    tasks.append((t + 1, 0, swap, (b, c, 1)))
                    tasks.append((t + 4, 0, parts_out, (b, c, 0)))
                    tasks.append((t + 8, 0, parts_out, (b, c, 1)))
                    for g in (2 * c, 2 * c + 1):
                        u = UPB * b + g
                        tasks.append((max(t + 9, STEPS * (u - 2) + 1), 1, stack, (u,)))
            for u in range(n_units):
                tasks.append((STEPS * u - 4.5, 2, max_row, (u,)))
                for half in range(2):
                    tasks.append((STEPS * u + 8 * (half + 1) + 1, 3, o_out, (2 * u + half,)))
            for b in range(nb):
                tasks.append((SPB * b + 36, 4, "y", (b,)))
                tasks.append((SPB * (b + 1) + 2, 4, den_in, (b,)))
                tasks.append((SPB * (b + 1) + 4, 4, den_out, (b,)))
                tasks.append((SPB * (b + 1) + 25, 5, "x1", (b,)))
                if b + 1 < nb:
                    tasks.append((SPB * b + 2, 6, "xt", (b + 1,)))
            tasks.sort(key=lambda x: (x[0], x[1]))
            for _, _, what, args in tasks:
                if what == "xt":
                    b, = args
                    wait(sp, s_fill, max(job_no[("K", (b - 1, 1, 1))], job_no[("V", (b - 1, KC // 2 - 1))]) + 1)
                    sp.dma_start(x_t[:, :, :], dram["x_t"][b]).then_inc(s_xt, 16)
                elif what == "y":
                    b, = args
                    if b:
                        wait(sp, s_x1, 16 * b)
                        wait(sp, s_fill, job_no[("T", (b - 1, KC // 2 - 1))] + 1)
                    sp.dma_start(y[:, :, :], dram["x"][b]).then_inc(s_y, 16)
                elif what == "x1":
                    b, = args
                    wait(sp, s_v, vec_done("norm", b))
                    sp.dma_start(dram["x1"][b * L:(b + 1) * L, :].rearrange("(t p) d -> p t d", p=P),
                                 y[:, :, :]).then_inc(s_x1, 16)
                else:
                    what(*args)
            wait(sp, s_x1, 16 * nb)
            wait(sp, s_blank, 16 * n_blank)
            wait(sp, s_cleared, 16)

        @block.gpsimd
        def _(pool):
            ones = [k_stack[i][ROWS:ROWS + NPART, :, :] for i in range(NSTK)] + [v[:, :, 1] for v in v_sb] + [ones_bf[:, :]]
            for i, dst in enumerate(ones):
                pool.memset(dst, 1.0).then_inc(s_ones, 1)
                pool.wait_ge(s_ones, i + 1)
            pool.memset(keep["blank"][:, :], 0.0).then_inc(s_zero, 1)
            done = [0]

            def step(ins, chained=True):
                ins.then_inc(s_pool, 1)
                done[0] += 1
                if chained:
                    pool.wait_ge(s_pool, done[0])

            wait(pool, s_par, 16 * 9)
            for _, name, args in todo_pool:
                assert done[0] == pool_no[(name, args)]
                if (name, args) == todo_pool[0][1:]:
                    done[0] += POOL_STEPS[name]
                    wait(pool, s_pool, done[0])
                elif name == "split":
                    done[0] = split(pool, *args, done[0])
                elif name == "bias_y":
                    b, = args
                    wait(pool, s_y, 16 * (b + 1))
                    step(pool.tensor_tensor(y[:, :, :], y[:, :, :],
                                            bo_row[:, :].unsqueeze(1).to_broadcast([P, KC, D]), ALU.add))
                elif name == "norm_o" and args == (nb - 1,):
                    done[0] += POOL_STEPS[name]
                elif name == "norm_o":
                    done[0] = norm_o(pool, *args, done[0])
                elif name == "list":
                    b, = args
                    wait(pool, s_v, vec_done("ranks", b))
                    wait(pool, s_cleared, 16)
                    list_tokens(pool, b, dram, keep)

        @block.scalar
        def _(act):
            def drain(n, name, args):
                if name not in ("Q", "K", "V", "T", "M"):
                    return
                wait(act, s_fill, n + 1)
                if name in ("Q", "K"):
                    b, c, half = args
                    which = "QK".index(name)
                    if n < 8:
                        wait(act, s_par, 16 * 9)
                    if half == 0 and (b, c) != (0, 0):
                        pb, pc = divmod(b * DC + c - 1, DC)
                        wait(act, s_pool, pool_done("split", pb, pc))
                    act.activation(feat[which][:, half * HALF:(half + 1) * HALF], ps_j[:, :], ACT.Identity,
                                   bias=bias[:, which, c:c + 1]).then_inc(s_drain, 1)
                elif name == "V":
                    b, i = args
                    wait(act, s_pv, SPB * (b - 1))
                    act.activation(v_sb[b % 2][:, 2 * i * D:(2 * i + 2) * D, 0], ps_j[:, :],
                                   ACT.Copy).then_inc(s_drain, 1)
                elif name == "T":
                    b, i = args
                    act.activation(x1_t[i % 2][:, :, :, :], ps_j[:, :].rearrange("p (a b c) -> p a b c", a=2, b=DC),
                                   ACT.Copy).then_inc(s_drain, 1)
                else:
                    u, = args
                    wait(act, s_mrow, 16 * NPART * u)
                    act.activation(max_rows[:, :], ps_j[:, :].bitcast(BF16)[0:NPART * G * KC, 0:P],
                                   ACT.Copy).then_inc(s_drain, 1)

            for t in range(first, steps_end):
                if 0 <= t < n_steps:
                    for pair in range(2):
                        wait(act, s_score, 2 * t + pair + 1)
                        wait(act, s_pv, t - 1)
                        act.activation(probs[t % 2][:, 2 * pair:2 * pair + 2, :], ps_b[pair][:, :, :], ACT.Exp,
                                       scale=float(DH) ** -0.5).then_inc(s_exp, 1)
                if 1 <= t <= n_steps and t % KC == 0:
                    n = t // KC - 1
                    wait(act, s_pv, t)
                    wait(act, s_oraw[n % 2], 16 * 2 * (n // 2))
                    act.activation(o_raw[n % 2][:, :], ps_o[:, :], ACT.Copy).then_inc(s_ocp, 1)
                for n, name, args in at_step.get(t, []):
                    drain(n, name, args)
                for b in range(nb):
                    if t == SPB * (b + 1) + 46:
                        wait(act, s_v, vec_done("top2", b))
                        act.activation(exps[:, :], shifted[:, :], ACT.Exp).then_inc(s_eexp, 1)

        @block.tensor
        def _(pe):
            def fill(n, name, args):
                wait(pe, s_drain, n)
                if name in ("Q", "K"):
                    b, c, half = args
                    if n < 8:
                        wait(pe, s_par, 16 * 9)
                    wait(pe, s_xt, 16 * (b + 1))
                    w = w_q if name == "Q" else w_k
                    for dc in range(DC):
                        ins = pe.matmul(ps_j[:, :], w[:, dc, c * P:(c + 1) * P], x_t[:, dc, half * HALF:(half + 1) * HALF],
                                        start=dc == 0, stop=dc == DC - 1)
                elif name == "V":
                    b, i = args
                    for a in range(2):
                        tok = (2 * i + a) * P
                        for dc in range(DC):
                            ins = pe.matmul(ps_j[:, a * D:(a + 1) * D], x_t[:, dc, tok:tok + P], w_v[:, dc, :],
                                            start=dc == 0, stop=dc == DC - 1)
                elif name == "M":
                    u, = args
                    wait(pe, s_v, vec_done("max_parts", u))
                    ins = pe.transpose(ps_j[:, :].bitcast(BF16)[0:NPART * G * KC, 0:P],
                                       max_parts[:, :, :].rearrange("p a b -> p (a b)"), ident_bf[:, :])
                elif name == "O":
                    b, i = args
                    wait(pe, s_pool, pool_done("norm_o", b))
                    for a in range(2):
                        tok = (2 * i + a) * P
                        for c in range(DC):
                            ins = pe.matmul(ps_j[:, a * D:(a + 1) * D], o_feat[b % 2][:, c, tok:tok + P], w_o[:, c, :],
                                            start=c == 0, stop=c == DC - 1)
                elif name == "T":
                    b, i = args
                    wait(pe, s_v, vec_done("norm", b))
                    for a in range(2):
                        for dc in range(DC):
                            at = (a * DC + dc) * P
                            ins = pe.transpose(ps_j[:, at:at + P], y[:, 2 * i + a, dc * P:(dc + 1) * P], con("ident"))
                elif name == "L":
                    b, i = args
                    for a in range(2):
                        for dc in range(DC):
                            ins = pe.matmul(ps_j[:, a * NG * NE:(a + 1) * NG * NE], x1_t[i % 2][:, a, dc, :],
                                            router[:, dc, :], start=dc == 0, stop=dc == DC - 1)
                else:
                    b, = args
                    wait(pe, s_v, vec_done("route", b))
                    lhs = ones_bf if name == "S" else tri_bf
                    for kk in range(TOPK):
                        ins = pe.matmul(ps_j[:, :], lhs[:, :], hot[kk][:, :, :, :].rearrange("p g t e -> p (g t e)"),
                                        start=kk == 0, stop=kk == TOPK - 1)
                ins.then_inc(s_fill, 1)

            def pv(t):
                u, s = divmod(t, STEPS)
                b, g = divmod(u, UPB)
                kc = s % KC
                wait(pe, s_exp, 2 * t + 2)
                if t % SPB == 0:
                    wait(pe, s_drain, job_no[("V", (b, KC // 2 - 1))] + 1)
                if kc == 0:
                    wait(pe, s_ocp, t // KC)
                v = v_sb[b % 2]
                for j in range(G):
                    at = kc * D + (g * G + j) * DH
                    ins = pe.matmul(ps_o[32 * j:32 * j + 32, :], v[:, at:at + DH, :].rearrange("p d s -> p (d s)"), probs[t % 2][:, j, :],
                                    start=kc == 0, stop=kc == KC - 1)
                ins.then_inc(s_pv, 1)

            def pass_a(ta, fills):
                u, i = divmod(ta, STEPS)
                if i == 0 and fills[0] == 0:
                    wait(pe, s_stack[u % NSTK], 16 * STACK_DMAS * (u // NSTK + 1))
                for f in fills:
                    fa = 4 * ta + f
                    hq = 2 * i + f // 2
                    j, qt, kh = hq // KC, hq % KC, f % 2
                    wait(pe, s_amax, fa - 1)
                    pe.matmul(ps_a[fa % 2][:, :], q_stack[u % NSTK][0:ROWS, j, qt * P:(qt + 1) * P],
                              k_stack[u % NSTK][0:ROWS, j, kh * HALF:(kh + 1) * HALF],
                              start=True, stop=True).then_inc(s_a, 1)

            wait(pe, s_ones, NSTK + 3)
            wait(pe, s_set, 3)
            for t in range(first, steps_end):
                ta = t + LEAD
                in_a = 0 <= ta < n_steps
                if 0 <= t < n_steps:
                    u, s = divmod(t, STEPS)
                    if s == 0:
                        wait(pe, s_mrow, 16 * NPART * (u + 1))
                    qh, kc = divmod(s, KC)
                    for pair in range(2):
                        if in_a:
                            pass_a(ta, (pair,))
                        wait(pe, s_exp, 2 * (t - 1) + pair + 1)
                        for jj in range(2):
                            j = 2 * pair + jj
                            ins = pe.matmul(ps_b[pair][:, jj, :], k_stack[u % NSTK][0:XROWS, j, kc * P:(kc + 1) * P],
                                            q_stack[u % NSTK][0:XROWS, j, qh * HALF:(qh + 1) * HALF],
                                            start=True, stop=True)
                        ins.then_inc(s_score, 1)
                elif in_a:
                    pass_a(ta, (0, 1))
                if in_a:
                    pass_a(ta, (2,))
                if 1 <= t <= n_steps:
                    pv(t - 1)
                if in_a:
                    pass_a(ta, (3,))
                for n, name, args in at_step.get(t, []):
                    fill(n, name, args)

        @block.vector
        def _(vec):
            done = [0]

            def drain(n, name, args):
                if name not in ("O", "L", "S", "R"):
                    return
                wait(vec, s_fill, n + 1)
                if name == "O":
                    b, i = args
                    wait(vec, s_pool, pool_done("bias_y", b))
                    yy = y[:, 2 * i:2 * i + 2, :]
                    vec.tensor_tensor(yy, ps_j[:, :].rearrange("p (a d) -> p a d", a=2), yy, ALU.add).then_inc(s_drain, 1)
                elif name == "L":
                    b, i = args
                    vec.tensor_copy(logits[:, 4 * i:4 * i + 4, :],
                                    ps_j[:, 0:2 * NG * NE].rearrange("p (a e) -> p a e", e=NE)).then_inc(s_drain, 1)
                elif name == "S":
                    vec.tensor_copy(totals[:, :].rearrange("p (g e t) -> p g t e", g=NG, t=KC),
                                    ps_j[:, :].rearrange("p (g t e) -> p g t e", g=NG, t=KC)).then_inc(s_drain, 1)
                else:
                    vec.tensor_copy(rank_of[:, :], ps_j[:, :]).then_inc(s_drain, 1)

            def ops_of(name, args):
                ops = []
                add = lambda emit, after=True: ops.append((emit, after))
                op = lambda after, call, *a, **kw: add(lambda: call(*a, **kw), after)
                if name == "max_parts":
                    u, = args

                    def first_op():
                        wait(vec, s_amax, 4 * STEPS * (u + 1))
                        if u:
                            wait(vec, s_fill, job_no[("M", (u - 1,))] + 1)
                        return vec.tensor_reduce(neg_max[:, :], maxima[u % 2][:, :, :], AX.X, ALU.max, negate=True)
                    add(first_op, False)
                    op(True, vec.tensor_copy, max_parts[:, 0, :], neg_max[:, :])
                    op(True, vec.tensor_tensor, max_rest[:, :], neg_max[:, :], max_parts[:, 0, :], ALU.subtract)
                    op(True, vec.tensor_copy, max_parts[:, 1, :], max_rest[:, :])
                    op(True, vec.tensor_tensor, max_parts[:, 2, :], max_rest[:, :], max_parts[:, 1, :], ALU.subtract)
                elif name == "recip":
                    b, = args

                    def first_op():
                        wait(vec, s_den, 16 * ((2 + H) * b + 1))
                        return vec.reciprocal(den[:, :], den[:, :])
                    add(first_op, False)
                elif name == "norm":
                    b, = args

                    def first_op():
                        wait(vec, s_drain, job_no[("O", (b, KC // 2 - 1))] + 1)
                        return vec.bn_stats(stats[:, 0, :], y[:, 0, :])
                    add(first_op, False)
                    for i in range(1, KC):
                        op(False, vec.bn_stats, stats[:, i, :], y[:, i, :])
                    for i in range(KC):
                        op(True, vec.bn_aggr, mean_var[:, i, :], stats[:, i, :])
                    inverse_root(vec, op, mean_var[:, :, 1], rstd, half_var, newton)
                    for i in range(KC):
                        op(True, vec.tensor_scalar, y[:, i, :], y[:, i, :], mean_var[:, i, 0:1], rstd[:, i:i + 1],
                           ALU.subtract, ALU.mult)
                elif name == "top2":
                    b, = args
                    n = KC * NG

                    def first_op():
                        wait(vec, s_drain, job_no[("L", (b, KC // 2 - 1))] + 1)
                        return vec.max(top_val[:, 0, :], logits[:, 0, :])
                    add(first_op, False)
                    for i in range(1, n):
                        op(False, vec.max, top_val[:, i, :], logits[:, i, :])
                    op(True, vec.tensor_tensor, shifted[:, 0:n * NE].rearrange("p (a e) -> p a e", e=NE), logits[:, :, :],
                       top_val[:, :, 0:1].to_broadcast([P, n, NE]), ALU.subtract)
                    op(False, vec.tensor_tensor, shifted[:, n * NE:], top_val[:, :, 1], top_val[:, :, 0], ALU.subtract)
                    for i in range(n):
                        op(False, vec.max_index, top_idx[:, i, :], top_val[:, i, :], logits[:, i, :])
                elif name == "route":
                    b, = args
                    n = KC * NG
                    tile = slice(b * KC, (b + 1) * KC)
                    by = lambda x: x.rearrange("p (t g) -> p g t", g=NG)

                    def first_op():
                        wait(vec, s_eexp, b + 1)
                        return vec.tensor_reduce(denom[:, :], exps[:, 0:n * NE].rearrange("p (a e) -> p a e", e=NE), AX.X, ALU.add)
                    add(first_op, False)
                    op(True, vec.reciprocal, denom[:, :], denom[:, :])
                    op(True, vec.tensor_scalar, keep["weight"][:, 0, :, tile], by(denom[:, :]), 0.5, None, ALU.mult)
                    op(True, vec.tensor_tensor, keep["weight"][:, 1, :, tile], by(exps[:, n * NE:]),
                       keep["weight"][:, 0, :, tile], ALU.mult)
                    for kk in range(TOPK):
                        op(False, vec.tensor_copy, keep["expert"][:, kk, :, tile], by(top_idx[:, :, kk]))
                    for kk in range(TOPK):
                        op(True, vec.tensor_tensor, hot[kk][:, :, :, :],
                           con("iota")[:, 0:NE].unsqueeze(1).unsqueeze(1).to_broadcast([P, NG, KC, NE]),
                           keep["expert"][:, kk, :, tile].unsqueeze(3).to_broadcast([P, NG, KC, NE]), ALU.is_equal)
                elif name == "ranks":
                    b, = args
                    tile = slice(b * KC, (b + 1) * KC)
                    get = lambda x: x.rearrange("p (g e t) -> p g e t", g=NG, t=KC)

                    def first_op():
                        wait(vec, s_drain, job_no[("R", (b,))] + 1)
                        return vec.tensor_tensor_scan(incl[:, :], con("scan"), totals[:, :], 0.0, ALU.mult, ALU.add)
                    add(first_op, False)
                    op(True, vec.tensor_tensor, totals[:, :], incl[:, :], totals[:, :], ALU.subtract)
                    op(True, vec.tensor_tensor, get(totals[:, :]), get(totals[:, :]),
                       keep["count"][:, :, :].unsqueeze(3).to_broadcast([P, NG, NE, KC]), ALU.add)
                    op(True, vec.tensor_tensor, keep["count"][:, :, :], keep["count"][:, :, :],
                       get(incl[:, :])[:, :, :, KC - 1], ALU.add)
                    rr = rank_of[:, :].rearrange("p (g t e) -> p g t e", g=NG, t=KC)
                    ii = incl[:, :].rearrange("p (g t e) -> p g t e", g=NG, t=KC)
                    op(True, vec.tensor_tensor, rr, rr, get(totals[:, :]).rearrange("p g e t -> p g t e"), ALU.add)
                    op(True, vec.tensor_tensor, ii, rr, hot[0][:, :, :, :], ALU.mult)
                    op(True, vec.tensor_tensor, rr, rr, hot[1][:, :, :, :], ALU.mult)
                    op(True, vec.tensor_reduce, keep["rank"][:, 0, :, tile], ii, AX.X, ALU.add)
                    op(False, vec.tensor_reduce, keep["rank"][:, 1, :, tile], rr, AX.X, ALU.add)

                    def place():
                        wait(vec, s_list, 16 * TOPK * KC * b)
                        return vec.scalar_tensor_tensor(listed[:, :, :], keep["expert"][:, :, 0, tile], float(nb * L),
                                                        keep["rank"][:, :, 0, tile], ALU.mult, ALU.add)
                    add(place, True)
                assert len(ops) == VEC_STEPS[name], (name, len(ops))
                return ops

            open_tasks, last_op = {}, {}

            def deal(t, slot):
                for name, args, i in vec_deal.get((t, slot), []):
                    key = (name, args)
                    if i == 0:
                        open_tasks[key] = ops_of(name, args)
                    emit, after = open_tasks[key][i]
                    if after:
                        wait(vec, s_v, last_op[key])
                    emit().then_inc(s_v, 1)
                    done[0] += 1
                    last_op[key] = done[0]

            vec.wait_ge(s_par, 16 * 9)
            vec.memset(keep["count"][:, :, :], 0.0).then_inc(s_set, 1)
            vec.tensor_scalar(keep["token"][:, :], con("iota")[:, 0:nb * KC], float(P), con("pid"), ALU.mult,
                              ALU.add)
            vec.tensor_copy(ident_bf[:, :], con("ident")).then_inc(s_set, 1)
            vec.tensor_copy(tri_bf[:, :], con("tri")).then_inc(s_set, 1)
            wait(vec, s_set, 3)
            split(vec, 0, 0, 0)
            for t in range(first, steps_end):
                if t == n_steps + 5:
                    wait(vec, s_pool, pool_no[("norm_o", (nb - 1,))])
                    norm_o(vec, nb - 1, pool_no[("norm_o", (nb - 1,))])
                ta = t + LEAD
                if 0 <= ta < n_steps:
                    u, i = divmod(ta, STEPS)
                    if i == 0 and u >= 2:
                        wait(vec, s_v, vec_done("max_parts", u - 2))
                    for f in range(4):
                        fa = 4 * ta + f
                        hq = 2 * i + f // 2
                        wait(vec, s_a, fa + 1)
                        vec.tensor_reduce(maxima[u % 2][:, hq, f % 2:f % 2 + 1], ps_a[fa % 2][:, :], AX.X,
                                          ALU.max).then_inc(s_amax, 1)
                        deal(t, f)
                else:
                    for slot in range(4):
                        deal(t, slot)
                for n, name, args in at_step.get(t, []):
                    drain(n, name, args)


def inverse_root(vec, op, var, rstd, half_var, scratch):
    op(True, vec.tensor_scalar, half_var[:, :], var, EPS, None, ALU.add)
    op(True, vec.tensor_scalar, rstd[:, :].bitcast(I32), half_var[:, :].bitcast(I32), 1, None, ALU.arith_shift_right)
    op(True, vec.tensor_scalar, rstd[:, :].bitcast(I32), rstd[:, :].bitcast(I32), -1.0, float(RSQRT_SEED), ALU.mult, ALU.add)
    for _ in range(3):
        op(True, vec.tensor_tensor, scratch[:, :], rstd[:, :], rstd[:, :], ALU.mult)
        op(True, vec.scalar_tensor_tensor, scratch[:, :], scratch[:, :], -0.5, half_var[:, :], ALU.mult, ALU.mult)
        op(True, vec.scalar_tensor_tensor, rstd[:, :], scratch[:, :], 1.5, rstd[:, :], ALU.add, ALU.mult)


def tables(tiles):
    cols, width = const_layout(tiles)
    out = np.zeros((P, width), np.float32)
    trig = np.zeros((P, 2, L), np.float32)
    put = lambda name, v: out.__setitem__((slice(None), slice(cols[name][0], cols[name][0] + cols[name][1])), v)
    inv_freq = (np.float32(1.0) / np.float32(10000.0) ** (np.arange(0, DH, 2, dtype=np.float32) / np.float32(DH))).astype(np.float32)
    angle = (np.arange(L, dtype=np.float32)[:, None] * inv_freq[None, :]).astype(np.float32).T
    dim = np.arange(P) // (P // DH)
    trig[:, 0] = np.cos(angle)[dim % (DH // 2)]
    trig[:, 1] = (np.sin(angle)[dim % (DH // 2)] * np.where(dim < DH // 2, np.float32(-1), np.float32(1))[:, None])
    put("ident", np.eye(P, dtype=np.float32))
    put("tri", np.triu(np.ones((P, P), np.float32), 1))
    put("iota", np.arange(cols["iota"][1], dtype=np.float32)[None, :])
    put("scan", (np.arange(NG * NE * KC) % KC != 0).astype(np.float32)[None, :])
    put("pid", np.arange(P, dtype=np.float32)[:, None])
    return out, trig


def host_arrays(inp, nb):
    x = np.ascontiguousarray(inp["attn_x"][:nb])
    by_dim = np.arange(D).reshape(DC, P // DH, DH).transpose(0, 2, 1).reshape(D)
    chunks = lambda w: np.ascontiguousarray(w.reshape(DC, P, -1).transpose(1, 0, 2))
    out = {
        "x_t": np.ascontiguousarray(x.transpose(0, 2, 1).reshape(nb, DC, P, L).transpose(0, 2, 1, 3)),
        "x": np.ascontiguousarray(x.reshape(nb, KC, P, D).transpose(0, 2, 1, 3)),
        "w_q": chunks(inp["attn_Wq"].T[:, by_dim]),
        "w_k": chunks(inp["attn_Wk"].T[:, by_dim]),
        "w_v": chunks(inp["attn_Wv"].T),
        "w_o": chunks(inp["attn_Wo"].T),
        "bias": np.ascontiguousarray(np.stack([inp["attn_bq"][by_dim], inp["attn_bk"][by_dim], inp["attn_bv"]])
                                     .reshape(3, DC, P).transpose(2, 0, 1)),
        "bo_row": np.ascontiguousarray(np.broadcast_to(inp["attn_bo"][None, :], (P, D))),
        "router": chunks(np.concatenate([inp["ffn_router_w0"], inp["ffn_router_w1"]], axis=1)),
    }
    out["consts"], out["trig"] = tables(n_tiles(nb * L))
    by_chunk = lambda w: w.reshape(NE, DC, P, HID).transpose(2, 0, 1, 3)
    for g in range(NG):
        out[f"w_gu{g}"] = np.ascontiguousarray(np.stack([by_chunk(inp[f"ffn_wg{g}"]), by_chunk(inp[f"ffn_wu{g}"])], axis=3))
        out[f"w_d{g}"] = np.ascontiguousarray(inp[f"ffn_wd{g}"].transpose(1, 0, 2))
    return out



def expert_phase(nc, nb, dram, keep, cols):
    tokens = nb * L
    NT = n_tiles(tokens)
    TT = nb * KC
    N = NG * NT
    NXG, NXT, NY, NXS, NID = 6, 3, 4, 4, 12
    NC = TOPK * NXS
    ACC_STEP = 10
    CHORE = 4
    PAIRS = TOPK * TT
    OWNER_STEPS = 18
    FETCH_LAG, ADD_LAG = 8, 13

    def spread_at(n):
        span = NT - 10
        part = lambda i: min(TT, max(0, i) * TT // span)
        return range(part(n), part(n + 1))

    def adds_at(n, lag):
        span = NT - 6 - ADD_LAG
        part = lambda i: min(PAIRS, max(0, i) * PAIRS // span)
        return range(part(n - NT - lag), part(n - NT - lag + 1))

    with ExitStack() as ctx:
        sb = lambda name, shape, dt=F32: ctx.enter_context(nc.sbuf_tensor(name + "_sb", shape, dt))
        ps = lambda name, shape: ctx.enter_context(nc.psum_tensor(name, shape, F32))
        sem = lambda name: ctx.enter_context(nc.semaphore(name))
        consts = keep["consts"]
        con = lambda name: consts[:, cols[name][0]:cols[name][0] + cols[name][1]]

        w_gu = [sb(f"w_gu{g}", [P, NE * DC * 2 * HID]) for g in range(NG)]
        w_d = sb("w_d", [P, NE * D])
        acc = w_gu[0][:, 0:TT * D].rearrange("p (t d) -> p t d", d=D)
        x_rows = [sb(f"x_rows{i}", [P, D + 2]) for i in range(NXG)]
        spread = [sb(f"spread{i}", [P, TOPK, D + 2]) for i in range(NXS)]
        meta = sb("meta", [P, TT, TOPK, 2])
        slot = sb("slot", [P, NT])
        place = [sb(f"place{i}", [P, 1], I32) for i in range(NY)]
        x_cols = [sb(f"x_cols{i}", [P, DC, P]) for i in range(NXT)]
        gate = [sb(f"gate{i}", [P, HID]) for i in range(2)]
        hidden = [sb(f"hidden{i}", [P, HID]) for i in range(2)]
        hidden_t = [sb(f"hidden_t{i}", [P, P]) for i in range(2)]
        y_rows = [sb(f"y_rows{i}", [P, D]) for i in range(NY)]
        back = [spread[i // TOPK][:, i % TOPK, 0:D] for i in range(NC)]
        NB = min(TT, NE * DC * 2 * HID // (TOPK * D))
        last = w_gu[1][:, 0:NB * TOPK * D].rearrange("p (n k d) -> p n k d", n=NB, k=TOPK)
        n_int = sb("n_int", [P, NG, NE], I32)
        n_fl, ends, ones_ne, base = (sb(n, [P, NG, NE]) for n in ("n_fl", "ends", "ones_ne", "base"))
        tile_id, owner = sb("tile_id", [P, 2]), sb("owner", [P, 2 * NG + 2])
        below = sb("below", [P, 2, NG, NE])
        owner_row = sb("owner_row", [2 * NG + 2, P], I32)
        own_n = sb("own_n", [P, 2, NE])
        start = sb("start", [P, 2])
        POS_CUTS = 4
        full = sb("full", [P, TT // POS_CUTS, NE])
        pos_f = sb("pos_f", [P, TOPK, TT])
        pos = sb("pos", [P, TOPK, NG, TT], I32)
        ids = sb("ids", [P, NT], I32)
        stats2, mean_var2 = sb("stats2", [P, 2, KC, 6]), sb("mean_var2", [P, 2, KC, 2])
        rstd2, half_var2, newton2, shift2 = (sb(n, [P, 2, KC]) for n in ("rstd2", "half_var2", "newton2", "shift2"))

        ps_x = [ps(f"ps_x{i}", [P, 2 * DC, P]) for i in range(2)]
        ps_g = [ps(f"ps_g{i}", [P, 512]) for i in range(2)]
        ps_h = ps("ps_h", [P, 512])
        ps_y = [ps(f"ps_y{i}", [P, 512]) for i in range(2)]
        ps_id = ps("ps_id", [P, 512])

        WCHUNK = 4
        WE = NE // WCHUNK
        s_wgu = [[sem(f"w_gu_in{g}_{c}") for c in range(WCHUNK)] for g in range(NG)]
        s_wd = [[sem(f"w_d_in{g}_{c}") for c in range(WCHUNK)] for g in range(NG)]
        s_route = sem("routing_step")
        s_tab, s_owner = sem("owners_transposed"), sem("owners_ready")
        s_ids = [sem(f"ids_in{i}") for i in range(NID)]
        s_gx = [sem(f"x_rows_in{i}") for i in range(NXG)]
        s_list_in = [sem(f"list_rows_in{i}") for i in range(NXG)]
        s_xt, s_xc = sem("x_transposed"), sem("x_cols_made")
        s_gu, s_silu, s_hid = sem("gate_up_done"), sem("gate_made"), sem("hidden_made")
        s_ht, s_htc, s_down, s_yr = sem("hidden_transposed"), sem("hidden_t_made"), sem("down_done"), sem("y_rows_made")
        s_yout = [sem(f"y_out{i}") for i in range(NY)]
        s_placed = [sem(f"y_placed{i}") for i in range(NY)]
        s_acc = [sem(f"acc_in{b}") for b in range(nb)]
        s_back = [sem(f"back_in{i}") for i in range(NC)]
        s_add = sem("row_added")
        s_xs = [sem(f"spread_in{i}") for i in range(NXS)]
        s_meta = sem("meta_made")
        s_list = [sem(f"listed{i}") for i in range(NXS)]
        s_last = [sem(f"last_in{i}") for i in range(NB)]
        s_both = sem("choices_added")
        s_norm, s_scales, s_fin, s_out = sem("norm_step"), sem("scales_ready"), sem("normalised"), sem("out_written")
        block = ctx.enter_context(nc.Block())

        def wait(eng, s, value):
            if value > 0:
                eng.wait_ge(s, value)

        def load_weights(sp, g, c):
            w = DC * 2 * HID
            sp.dma_start(w_gu[g][:, c * WE * w:(c + 1) * WE * w],
                         dram[f"w_gu{g}"][:, c * WE:(c + 1) * WE].rearrange("p e c s h -> p (e c s h)")).then_inc(s_wgu[g][c], 16)

        def load_down(sp, g, c):
            sp.dma_start(w_d[:, c * WE * D:(c + 1) * WE * D],
                         dram[f"w_d{g}"][:, c * WE:(c + 1) * WE].rearrange("p e d -> p (e d)")).then_inc(s_wd[g][c], 16)

        def weights_at(i):
            return [i // WE] if i % WE == 0 and i < NE else []

        def store_y(sp, n):
            wait(sp, s_yr, n + 1)
            sp.dma_start(dram["y"][0][n * P:(n + 1) * P, :], y_rows[n % NY][:, :]).then_inc(s_yout[n % NY], 16)

        W0_FIRST = 2
        W0_AT = [2 * c for c in range(WCHUNK - W0_FIRST)]
        W1_AT = [12 + 4 * c for c in range(WCHUNK)]

        def spread_out(eng, t):
            if t >= 0:
                wait(eng, s_list[t % NXS], 16 * TOPK * (t // NXS + 1))

        def load_ids(sp, n):
            if n == 0:
                wait(sp, s_owner, 1)
                wait(sp, keep["s_list"], 16 * TOPK * KC * nb)
            if n >= NID:
                wait(sp, s_ids[n % NID], 16 * (n // NID))
            row = 2 * NG + n // P
            at = sp.value_load(owner_row[row:row + 1, n % P:n % P + 1], min_val=0, max_val=NE * tokens - P)
            sp.dma_start(ids[:, n:n + 1], dram["list"][bass.ds(at, P), :]).then_inc(s_ids[n % NID], 16)

        def load_spread(sp, t):
            spread_out(sp, t - NXS)
            sp.dma_start(spread[t % NXS][:, :, 0:D],
                         dram["x1"][t * P:(t + 1) * P, :].unsqueeze(1).to_broadcast([P, TOPK, D])).then_inc(s_xs[t % NXS], 16)

        def load_rows(sp, n):
            if n == NT:
                for t in range(TT - NXS, TT):
                    spread_out(sp, t)
            wait(sp, s_yr, n - NXG + 1)
            sp.dma_start(x_rows[n % NXG][:, :], dram["rows"][(n - NT) * P:(n - NT + 1) * P, :]
                         ).then_inc(s_list_in[n % NXG], 16)

        def load_last(sp, t):
            if t >= NB:
                wait(sp, s_add, PAIRS + t - NB + 1)
            lo = NT * P + t * P * TOPK
            sp.dma_start(last[:, t % NB, :, :],
                         dram["y"][1][lo:lo + P * TOPK, :].rearrange("(p k) d -> p k d", k=TOPK)).then_inc(s_last[t % NB], 16)

        def y_left(eng, n):
            if n >= NT:
                wait(eng, s_placed[n % NY], 16 * len(range(NT + (n - NT) % NY, n + 1, NY)))
            elif n >= 0:
                wait(eng, s_yout[n % NY], 16 * (n // NY + 1))

        def stored(eng, g):
            for i in range(NY):
                y_left(eng, NT * (g + 1) - 1 - i)

        adds = [(0, t, kk) for t in range(TT) for kk in range(TOPK)]

        @block.sync
        def _(sp):
            for c in range(W0_FIRST):
                load_weights(sp, 0, c)
                load_down(sp, 0, c)
            for n in range(NID):
                load_ids(sp, n)
            for t in range(NXS):
                load_spread(sp, t)
            for n in range(N):
                if n < NT:
                    store_y(sp, n)
                    if n + NID < NT:
                        load_ids(sp, n + NID)
                    for t in spread_at(n - 4):
                        if t + NXS < TT:
                            load_spread(sp, t + NXS)
                if NT <= n + NXG < N:
                    load_rows(sp, n + NXG)
                if n in W0_AT:
                    load_weights(sp, 0, W0_FIRST + W0_AT.index(n))
                    load_down(sp, 0, W0_FIRST + W0_AT.index(n))
                if n in W1_AT:
                    load_weights(sp, 1, W1_AT.index(n))
                if n == NT - 1:
                    wait(sp, s_down, NT)
                    for c in range(WCHUNK):
                        load_down(sp, 1, c)
                for b in range(nb):
                    if n == NT + 2 + ACC_STEP * b:
                        if b == 0:
                            wait(sp, s_gu, NT)
                        sp.dma_start(acc[:, b * KC:(b + 1) * KC, :],
                                     dram["x1"][b * L:(b + 1) * L, :].rearrange("(t p) d -> p t d", p=P)).then_inc(s_acc[b], 16)
            stored(sp, 1)
            for t in range(TT):
                load_last(sp, t)

        @block.gpsimd
        def _(pool):
            def gather(n):
                wait(pool, s_ids[n % NID], 16 * (n // NID + 1))
                wait(pool, s_xt, n - NXG + 1)
                pool.indirect_dma_start(x_rows[n % NXG][:, 0:D], None, dram["x1"][:, :],
                                        bass.IndirectOffsetOnAxis(ap=ids[:, n:n + 1], axis=0)).then_inc(s_gx[n % NXG], 16)

            def spread_rows(t):
                wait(pool, s_xs[t % NXS], 16 * (t // NXS + 1))
                wait(pool, s_meta, t + 1)
                for kk in range(TOPK):
                    pool.indirect_dma_start(dram["rows"], bass.IndirectOffsetOnAxis(ap=pos[:, kk, 1, t:t + 1], axis=0),
                                            spread[t % NXS][:, kk, :], None).then_inc(s_list[t % NXS], 16)

            def place_y(n):
                wait(pool, s_yr, n + 1)
                pool.indirect_dma_start(dram["y"][1], bass.IndirectOffsetOnAxis(ap=place[n % NY][:, :], axis=0),
                                        y_rows[n % NY][:, :], None).then_inc(s_placed[n % NY], 16)

            def fetch(a):
                g, t, kk = adds[a]
                if a == 0:
                    stored(pool, 0)
                    for i in range(TT - NXS, TT):
                        spread_out(pool, i)
                wait(pool, s_add, a - NC + 1)
                pool.indirect_dma_start(back[a % NC], None, dram["y"][g],
                                        bass.IndirectOffsetOnAxis(ap=pos[:, kk, g, t:t + 1], axis=0)).then_inc(s_back[a % NC], 16)

            list_tokens(pool, nb - 1, dram, keep)
            for n in range(NT):
                gather(n)
                for t in spread_at(n - NXG):
                    spread_rows(t)
            for n in range(NT, N + 2):
                if n - 2 >= NT:
                    place_y(n - 2)
                for a in adds_at(n, FETCH_LAG):
                    fetch(a)
            for t in range(TT):
                wait(pool, s_last[t % NB], 16 * (t // NB + 1))
                pool.tensor_tensor(last[:, t % NB, 0, :], last[:, t % NB, 0, :], last[:, t % NB, 1, :],
                                   ALU.add).then_inc(s_both, 1)

        @block.scalar
        def _(act):
            def columns(n):
                wait(act, s_xt, n + 1)
                wait(act, s_gu, n - NXT + 1)
                act.activation(x_cols[n % NXT][:, :, :], ps_x[n % 2][:, 0:DC, :], ACT.Copy).then_inc(s_xc, 1)

            for n in range(-1, N):
                if n >= 0:
                    wait(act, s_gu, n + 1)
                    wait(act, s_hid, n - 1)
                    act.activation(gate[n % 2][:, :], ps_g[n % 2][:, 0:HID], ACT.Silu).then_inc(s_silu, 1)
                for m in ((0, 1) if n == -1 else (n + 2,)):
                    if m < N:
                        columns(m)
            for b in range(nb):
                wait(act, s_scales, b + 1)
                for i in range(KC):
                    t = b * KC + i
                    act.activation(acc[:, t, :], acc[:, t, :], ACT.Identity, bias=shift2[:, b % 2, i:i + 1],
                                   scale=rstd2[:, b % 2, i:i + 1]).then_inc(s_fin, 1)
                wait(act, s_fin, KC * (b + 1))
                act.dma_start(dram["out"][b].rearrange("(t p) d -> p t d", p=P),
                              acc[:, b * KC:(b + 1) * KC, :]).then_inc(s_out, 16)
            act.wait_ge(s_out, 16 * nb)

        @block.tensor
        def _(pe):
            def owners():
                wait(pe, s_route, OWNER_STEPS)
                pe.transpose(ps_id[0:2 * NG + 2, 0:P], owner[:, :], con("ident")).then_inc(s_tab, 1)

            def transpose_x(n):
                if n < NT:
                    wait(pe, s_gx[n % NXG], 16 * (n // NXG + 1))
                else:
                    wait(pe, s_list_in[n % NXG], 16 * len(range(NT + (n - NT) % NXG, n + 1, NXG)))
                wait(pe, s_xc, n - 1)
                for dc in range(DC):
                    ins = pe.transpose(ps_x[n % 2][:, dc, :], x_rows[n % NXG][:, dc * P:(dc + 1) * P], con("ident"))
                ins.then_inc(s_xt, 1)

            def gate_up(n, e):
                g, i = divmod(n, NT)
                for c in weights_at(i):
                    wait(pe, s_wgu[g][c], 16)
                wait(pe, s_xc, n + 1)
                wait(pe, s_hid, n - 1)
                for dc in range(DC):
                    ins = pe.matmul(ps_g[n % 2][:, 0:2 * HID], x_cols[n % NXT][:, dc, :],
                                    w_gu[g][:, bass.ds(e * (DC * 2 * HID) + dc * 2 * HID, 2 * HID)],
                                    start=dc == 0, stop=dc == DC - 1)
                ins.then_inc(s_gu, 1)

            def transpose_h(n):
                wait(pe, s_hid, n + 1)
                wait(pe, s_htc, n)
                pe.transpose(ps_h[:, 0:P], hidden[n % 2][:, :], con("ident")).then_inc(s_ht, 1)

            def down(n, e):
                g, i = divmod(n, NT)
                for c in weights_at(i):
                    wait(pe, s_wd[g][c], 16)
                wait(pe, s_htc, n + 1)
                wait(pe, s_yr, n - 1)
                pe.matmul(ps_y[n % 2][:, 0:D], hidden_t[n % 2][:, :], w_d[:, bass.ds(e * D, D)],
                          start=True, stop=True).then_inc(s_down, 1)

            owners()
            wait(pe, s_owner, 1)
            expert = {}
            for n in range(N + 2):
                if n == 0:
                    transpose_x(0)
                    transpose_x(1)
                if n < N:
                    g, i = divmod(n, NT)
                    row = (i // P) * NG + g
                    expert[n] = pe.value_load(owner_row[row:row + 1, i % P:i % P + 1], min_val=0, max_val=NE - 1)
                    gate_up(n, expert[n])
                if 1 <= n <= N:
                    transpose_h(n - 1)
                if 2 <= n:
                    down(n - 2, expert.pop(n - 2))
                if n + 2 < N:
                    transpose_x(n + 2)

        @block.vector
        def _(vec):
            done = [0]

            def step(ins, chained=True):
                ins.then_inc(s_route, 1)
                done[0] += 1
                if chained:
                    vec.wait_ge(s_route, done[0])

            def positions(g):
                n = TT // POS_CUTS
                for kk in range(TOPK):
                    for i in range(POS_CUTS):
                        tiles = slice(i * n, (i + 1) * n)
                        step(vec.tensor_tensor(full[:, :, :], con("iota")[:, 0:NE].unsqueeze(1).to_broadcast([P, n, NE]),
                                               keep["expert"][:, kk, g, tiles].unsqueeze(2).to_broadcast([P, n, NE]), ALU.is_equal))
                        yield
                        step(vec.tensor_tensor(full[:, :, :], full[:, :, :],
                                               base[:, g, :].unsqueeze(1).to_broadcast([P, n, NE]), ALU.mult))
                        yield
                        step(vec.tensor_reduce(pos_f[:, kk, tiles], full[:, :, :], AX.X, ALU.add))
                        yield
                step(vec.tensor_tensor(pos_f[:, :, :], pos_f[:, :, :], keep["rank"][:, :, g, :], ALU.add))
                yield
                step(vec.tensor_copy(pos[:, :, g, :], pos_f[:, :, :]))
                yield

            def metas():
                place_t = meta[:, :, :, 0]
                step(vec.tensor_scalar(tile_id[:, 0:1], con("pid"), float(TOPK), float(NT * P), ALU.mult, ALU.add))
                for kk in range(TOPK):
                    step(vec.tensor_scalar(place_t[:, :, kk], con("iota")[:, 0:TT], float(TOPK * P), tile_id[:, 0:1],
                                           ALU.mult, ALU.add), chained=kk == TOPK - 1)
                step(vec.tensor_scalar(place_t[:, :, 1], place_t[:, :, 1], 1.0, None, ALU.add))
                step(vec.tensor_copy(meta[:, :, :, 1], keep["weight"][:, :, 1, :].rearrange("p k t -> p t k")))
                step(vec.tensor_scalar(slot[:, :], con("iota")[:, 0:NT], float(P), con("pid"), ALU.mult, ALU.add))

            def mark(t):
                spread_out(vec, t - NXS)
                vec.tensor_copy(spread[t % NXS][:, :, D:D + 2], meta[:, t, :, :]).then_inc(s_meta, 1)

            step(vec.memset(ones_ne[:, :, :], 1.0), chained=False)
            step(vec.tensor_scalar(n_int[:, :, :], keep["count"][:, :, :], float(P - 1), None, ALU.add))
            step(vec.tensor_scalar(n_int[:, :, :], n_int[:, :, :], 7, None, ALU.arith_shift_right))
            step(vec.tensor_copy(n_fl[:, :, :], n_int[:, :, :]))
            for g in range(NG):
                ins = vec.tensor_tensor_scan(ends[:, g, :], ones_ne[:, g, :], n_fl[:, g, :], 0.0, ALU.mult, ALU.add)
                step(ins, chained=g == NG - 1)
            for hi in range(2):
                step(vec.tensor_scalar(tile_id[:, hi:hi + 1], con("pid"), float(hi * P), None, ALU.add), chained=hi == 1)
            for hi in range(2):
                step(vec.tensor_tensor(below[:, hi, :, :], ends[:, :, :],
                                       tile_id[:, hi:hi + 1].unsqueeze(2).to_broadcast([P, NG, NE]), ALU.is_le),
                     chained=hi == 1)
            step(vec.tensor_reduce(owner[:, 0:2 * NG].rearrange("p (h g) -> p h g", h=2), below[:, :, :, :], AX.X, ALU.add))
            step(vec.tensor_scalar(owner[:, 0:2 * NG], owner[:, 0:2 * NG], float(NE - 1), None, ALU.min))
            step(vec.tensor_tensor(own_n[:, :, :], below[:, :, 0, :], n_fl[:, 0, :].unsqueeze(1).to_broadcast([P, 2, NE]),
                                   ALU.mult))
            step(vec.tensor_reduce(start[:, :], own_n[:, :, :], AX.X, ALU.add))
            step(vec.tensor_tensor(start[:, :], tile_id[:, :], start[:, :], ALU.subtract))
            step(vec.tensor_scalar(start[:, :], start[:, :], float(P), None, ALU.mult))
            step(vec.scalar_tensor_tensor(start[:, :], owner[:, 0:2 * NG:NG], float(tokens), start[:, :], ALU.mult, ALU.add))
            step(vec.tensor_scalar(owner[:, 2 * NG:2 * NG + 2], start[:, :], float(NE * tokens - P), None, ALU.min))
            assert done[0] == OWNER_STEPS
            step(vec.tensor_tensor(base[:, :, :], ends[:, :, :], n_fl[:, :, :], ALU.subtract))
            step(vec.tensor_scalar(base[:, :, :], base[:, :, :], float(P), None, ALU.mult))
            wait(vec, s_tab, 1)
            vec.tensor_copy(owner_row[:, :], ps_id[0:2 * NG + 2, 0:P]).then_inc(s_owner, 1)
            for _ in positions(1):
                pass
            metas()

            chores = positions(0)

            def tile_work(n):
                if n < N:
                    wait(vec, s_silu, n + 1)
                    wait(vec, s_ht, n - 1)
                    vec.tensor_tensor(hidden[n % 2][:, :], gate[n % 2][:, :], ps_g[n % 2][:, HID:2 * HID],
                                      ALU.mult).then_inc(s_hid, 1)
                if 1 <= n <= N:
                    m = n - 1
                    wait(vec, s_ht, m + 1)
                    wait(vec, s_down, m - 1)
                    vec.tensor_copy(hidden_t[m % 2][:, :], ps_h[:, 0:P]).then_inc(s_htc, 1)
                if 2 <= n:
                    m = n - 2
                    wait(vec, s_down, m + 1)
                    y_left(vec, m - NY)
                    if m < NT:
                        vec.tensor_copy(y_rows[m % NY][:, :], ps_y[m % 2][:, 0:D]).then_inc(s_yr, 1)
                    else:
                        row = x_rows[m % NXG]
                        vec.tensor_tensor(place[m % NY][:, :], row[:, D:D + 1], slot[:, m - NT:m - NT + 1], ALU.max)
                        vec.tensor_scalar(y_rows[m % NY][:, :], ps_y[m % 2][:, 0:D], row[:, D + 1:D + 2], None,
                                          ALU.mult).then_inc(s_yr, 1)

            def add(a):
                g, t, kk = adds[a]
                wait(vec, s_acc[t // KC], 16)
                wait(vec, s_back[a % NC], 16 * (a // NC + 1))
                wait(vec, s_add, a)
                vec.scalar_tensor_tensor(acc[:, t, :], back[a % NC], keep["weight"][:, kk, g, t:t + 1], acc[:, t, :],
                                         ALU.mult, ALU.add).then_inc(s_add, 1)

            for n in range(N + 2):
                tile_work(n)
                if CHORE <= n < NT:
                    next(chores, None)
                if n < NT:
                    for t in spread_at(n):
                        mark(t)
                for a in adds_at(n, ADD_LAG):
                    add(a)
            norms = [0]

            def scales(b):
                two = b % 2
                stats, mean_var, rstd, shift = stats2[:, two], mean_var2[:, two], rstd2[:, two], shift2[:, two]
                wait(vec, s_fin, KC * (b - 1))
                wait(vec, s_norm, norms[0])
                for i in range(KC):
                    vec.bn_aggr(mean_var[:, i, :], stats[:, i, :]).then_inc(s_norm, 1)
                    norms[0] += 1
                    yield
                ops = []
                inverse_root(vec, lambda after, call, *a: ops.append((call, a)), mean_var[:, :, 1], rstd,
                             half_var2[:, two], newton2[:, two])
                ops.append((vec.scalar_tensor_tensor, (shift[:, :], mean_var[:, :, 0], -1.0, rstd[:, :], ALU.mult, ALU.mult)))
                before = norms[0]
                for n, (call, a) in enumerate(ops):
                    wait(vec, s_norm, before)
                    ins = call(*a)
                    if n < len(ops) - 1:
                        ins.then_inc(s_norm, 1)
                        norms[0] += 1
                        before = norms[0]
                    else:
                        ins.then_inc(s_scales, 1)
                    yield

            def statistics(t):
                b, i = divmod(t, KC)
                wait(vec, s_add, PAIRS + t + 1)
                vec.bn_stats(stats2[:, b % 2, i, :], acc[:, t, :]).then_inc(s_norm, 1)
                norms[0] += 1

            making = iter(())
            wait(vec, s_add, PAIRS)
            for t in range(TT):
                wait(vec, s_both, t + 1)
                vec.tensor_tensor(acc[:, t, :], acc[:, t, :], last[:, t % NB, 0, :], ALU.add).then_inc(s_add, 1)
                for _ in range(3):
                    next(making, None)
                if t % KC:
                    statistics(t - 1)
                if t % KC == KC - 1:
                    statistics(t)
                    for _ in making:
                        pass
                    making = scales(t // KC)
            for _ in making:
                pass


def build(nc, nb, a):
    tokens = nb * L
    cols, width = const_layout(n_tiles(tokens))
    with ExitStack() as ctx:
        sb = lambda name, shape, dt=F32: ctx.enter_context(nc.sbuf_tensor(name + "_sb", shape, dt))
        keep = {
            "rank": sb("rank", [P, TOPK, NG, nb * KC]),
            "expert": sb("expert", [P, TOPK, NG, nb * KC]),
            "weight": sb("weight", [P, TOPK, NG, nb * KC]),
            "count": sb("count", [P, NG, NE]),
            "consts": sb("consts", [P, width]),
            "blank": sb("blank", [P, D + 2]),
            "token": sb("token", [P, nb * KC], I32),
            "listed": sb("listed", [P, TOPK, KC], I32),
            "s_list": ctx.enter_context(nc.semaphore("tokens_listed")),
        }
        dram = dict(a)
        dram["parts"] = nc.dram_tensor("parts_dram", [nb * DC, 2, NPART, P, L], BF16, kind="Internal").ap()
        dram["den"] = nc.dram_tensor("den_dram", [nb, H, L], F32, kind="Internal").ap()
        dram["inv"] = nc.dram_tensor("inv_dram", [nb, H, L], F32, kind="Internal").ap()
        listed = n_tiles(tokens) * P
        dram["list"] = nc.dram_tensor("list_dram", [NE * tokens, 1], I32, kind="Internal").ap()
        dram["rows"] = nc.dram_tensor("rows_dram", [listed, D + 2], F32, kind="Internal").ap()
        dram["y"] = [nc.dram_tensor(f"y_dram{g}", [listed + g * tokens * TOPK, D], F32, kind="Internal").ap()
                     for g in range(NG)]
        dram["x1"] = nc.dram_tensor("x1_dram", [tokens, D], F32, kind="Internal").ap()
        attention_phase(nc, nb, dram, keep, cols)
        expert_phase(nc, nb, dram, keep, cols)


def kernel(**inputs):
    import concourse.bacc as bacc
    from concourse.bass_utils import run_bass_kernel_spmd

    arrays = host_arrays({name[3:]: np.asarray(v) for name, v in inputs.items()}, 8)
    nb = arrays["x"].shape[0]
    nc = bacc.Bacc("TRN2", target_bir_lowering=False, num_devices=1)
    args = {name: nc.dram_tensor(name, v.shape, mybir.dt.from_np(v.dtype), kind="ExternalInput").ap()
            for name, v in arrays.items()}
    args["out"] = nc.dram_tensor("out", (nb, L, D), F32, kind="ExternalOutput").ap()
    build(nc, nb, args)
    return run_bass_kernel_spmd(nc, [arrays], core_ids=[0]).results[0]["out"]
```
